# Optimizing a Trainium2 kernel written in Bass

```python
import numpy as np
import jax
import jax.numpy as jnp

def _softmax(x, axis=-1):
    return jax.nn.softmax(x, axis=axis)

def _gelu(x):
    return jax.nn.gelu(x, approximate=True)

def _silu(x):
    return jax.nn.silu(x)

def _sigmoid(x):
    return jax.nn.sigmoid(x)

def _layernorm(x, axis=-1, eps=1e-05):
    m = jnp.mean(x, axis=axis, keepdims=True)
    v = jnp.var(x, axis=axis, keepdims=True)
    return (x - m) / jnp.sqrt(v + eps)

def _scatter_add(tgt, idx, src, axis=0):
    return tgt.at[idx].add(src)

def _segment_sum(src, seg, n):
    return jax.ops.segment_sum(src, seg, n)
kernel_name = 'mk_flamingo_gated_d1_seqx_r2_df3764'

def setup_inputs(seed: int=0):
    np.random.seed(seed)
    _w = jnp.asarray

    def _rec_inputs():
        import jax
        import jax.numpy as jnp
        _rk = jax.random.key(seed)
        x = 7.22e-05 + 1 * jax.random.normal(jax.random.fold_in(_rk, 1), (16, 256, 512), jnp.float32)
        _lenS = 256 - jax.random.randint(jax.random.fold_in(_rk, 7), (16,), 0, max(1, 256 // 4) + 1, jnp.int32)
        _lenS2 = 256 - jax.random.randint(jax.random.fold_in(_rk, 8), (16,), 0, max(1, 256 // 4) + 1, jnp.int32)
        _ctx_1024P = jax.random.normal(jax.random.fold_in(_rk, 11), (16, 16, 512), jnp.float32)
        _ctx_1024c = jax.random.dirichlet(jax.random.fold_in(_rk, 511), 0.3 * jnp.ones((16,), jnp.float32), (16, 256))
        _ctx_1024t = jnp.einsum('bsk,bkd->bsd', _ctx_1024c, _ctx_1024P)
        _ctx_1024t = _ctx_1024t * jax.lax.rsqrt(jnp.mean(jnp.square(_ctx_1024t)) + 1e-12) * 0.953939
        ctx_1024 = 4.13588e-05 + 0.999923 * (_ctx_1024t + 0.3 * jax.random.normal(jax.random.fold_in(_rk, 611), (16, 256, 512), jnp.float32))
        _g = jax.random.normal(jax.random.fold_in(_rk, 9001), (2, 1), jnp.float32)
        _g = jnp.sign(_g) * jnp.maximum(jnp.abs(_g), 1.0) + (_g == 0) * 1.0
        g_xattn = _g[0]
        g_ffn = _g[1]
        return (x, ctx_1024, g_xattn, g_ffn)
    x, ctx_1024, g_xattn, g_ffn = _rec_inputs()

    def _L0_xattn_setup():
        import jax, jax.numpy as jnp
        import numpy as np
        EMBED_DIM = 512
        B, QL, KL = (4, 1024, 1024)
        key = jax.random.key(seed)
        k1, k2, k3, k4 = jax.random.split(key, 4)
        hidden_states = jax.random.normal(k1, (B, QL, EMBED_DIM), dtype=jnp.float32)
        decoder_hidden_states = jax.random.normal(k2, (B, KL, EMBED_DIM), dtype=jnp.float32)
        Wq = jax.random.normal(k3, (EMBED_DIM, EMBED_DIM), dtype=jnp.float32) * (1.0 / np.sqrt(EMBED_DIM))
        Wkv = jax.random.normal(k4, (EMBED_DIM, 2 * EMBED_DIM), dtype=jnp.float32) * (1.0 / np.sqrt(EMBED_DIM))
        return {'hidden_states': hidden_states, 'decoder_hidden_states': decoder_hidden_states, 'Wq': Wq, 'Wkv': Wkv}
    _L0_xattn_all = _L0_xattn_setup()
    _L0_xattn_in = {k: v for k, v in _L0_xattn_all.items() if k in ('Wq', 'Wkv')}
    del _L0_xattn_all

    def _L0_ffn_setup():
        import jax, jax.numpy as jnp
        import numpy as np
        K = 2
        key = jax.random.key(seed)
        ks = jax.random.split(key, 9)
        B, S, D, O, E = (4, 512, 512, 512, 8)
        sc = 0.02
        return {'x': jax.random.normal(ks[0], (B, S, D), dtype=jnp.float32), 'gate_w': jax.random.normal(ks[1], (D, E), dtype=jnp.float32) * sc, 'gate_b': jax.random.normal(ks[2], (E,), dtype=jnp.float32) * sc, 'w1': jax.random.normal(ks[3], (E, D, O), dtype=jnp.float32) * sc, 'b1': jax.random.normal(ks[4], (E, O), dtype=jnp.float32) * sc, 'w2': jax.random.normal(ks[5], (E, O, O), dtype=jnp.float32) * sc, 'b2': jax.random.normal(ks[6], (E, O), dtype=jnp.float32) * sc, 'w3': jax.random.normal(ks[7], (E, O, O), dtype=jnp.float32) * sc, 'b3': jax.random.normal(ks[8], (E, O), dtype=jnp.float32) * sc}
    _L0_ffn_all = _L0_ffn_setup()
    _L0_ffn_in = {k: v for k, v in _L0_ffn_all.items() if k in ('gate_w', 'gate_b', 'w1', 'b1', 'w2', 'b2', 'w3', 'b3')}
    del _L0_ffn_all
    return {'x': x, 'ctx_1024': ctx_1024, 'g_xattn': g_xattn, 'g_ffn': g_ffn, 'L0_xattn_Wq': _L0_xattn_in['Wq'], 'L0_xattn_Wkv': _L0_xattn_in['Wkv'], 'L0_ffn_gate_w': _L0_ffn_in['gate_w'], 'L0_ffn_gate_b': _L0_ffn_in['gate_b'], 'L0_ffn_w1': _L0_ffn_in['w1'], 'L0_ffn_b1': _L0_ffn_in['b1'], 'L0_ffn_w2': _L0_ffn_in['w2'], 'L0_ffn_b2': _L0_ffn_in['b2'], 'L0_ffn_w3': _L0_ffn_in['w3'], 'L0_ffn_b3': _L0_ffn_in['b3']}

def reference(x, ctx_1024, g_xattn, g_ffn, L0_xattn_Wq, L0_xattn_Wkv, L0_ffn_gate_w, L0_ffn_gate_b, L0_ffn_w1, L0_ffn_b1, L0_ffn_w2, L0_ffn_b2, L0_ffn_w3, L0_ffn_b3):
    import jax
    import jax.numpy as jnp

    def _L0_xattn_ref(hidden_states, decoder_hidden_states, Wq, Wkv):
        import jax, jax.numpy as jnp
        import numpy as np
        EMBED_DIM = 512
        B, QL, KL = (4, 1024, 1024)
        d = Wq.shape[0]
        scale = 1.0 / np.sqrt(d)
        query = hidden_states @ Wq
        kv = decoder_hidden_states @ Wkv
        key, value = jnp.split(kv, 2, axis=-1)
        scores = jnp.einsum('bqd,bkd->bqk', query, key) * scale
        w = jax.nn.softmax(scores, axis=-1)
        return jnp.einsum('bqk,bkd->bqd', w, value)

    def _L0_ffn_ref(x, gate_w, gate_b, w1, b1, w2, b2, w3, b3):
        import jax, jax.numpy as jnp
        import numpy as np
        K = 2
        E = gate_w.shape[-1]
        logits = jnp.einsum('bsd,de->bse', x, gate_w) + gate_b
        probs = jax.nn.softmax(logits, axis=1)
        vals, idx = jax.lax.top_k(probs, K)
        h = jax.nn.relu(jnp.einsum('bsd,edo->ebso', x, w1) + b1[:, None, None, :])
        h = jax.nn.relu(jnp.einsum('ebso,eop->ebsp', h, w2) + b2[:, None, None, :])
        y = jax.nn.relu(jnp.einsum('ebso,eop->ebsp', h, w3) + b3[:, None, None, :])
        onehot = jax.nn.one_hot(idx, E, dtype=x.dtype)
        w_tok = jnp.einsum('bske,bsk->bse', onehot, vals)
        ind = onehot.max(axis=2)
        v = jnp.einsum('ebso,bse->eo', y, w_tok)
        out = jnp.einsum('bse,eo->bso', ind, v)
        return out
    x = x + jnp.tanh(g_xattn[0]) * _L0_xattn_ref(_layernorm(x, axis=-1), ctx_1024, L0_xattn_Wq, L0_xattn_Wkv)
    x = x + jnp.tanh(g_ffn[0]) * _L0_ffn_ref(_layernorm(x, axis=-1), L0_ffn_gate_w, L0_ffn_gate_b, L0_ffn_w1, L0_ffn_b1, L0_ffn_w2, L0_ffn_b2, L0_ffn_w3, L0_ffn_b3)
    return x

_drawn_inputs = setup_inputs


def setup_inputs(seed=0):
    import zlib

    import numpy as np

    out = dict(_drawn_inputs(seed))
    spreads = {}
    factors = {'L0_ffn_gate_b': 64.0, 'L0_ffn_w1': 3.963, 'L0_ffn_b1': 8.0, 'L0_ffn_b2': 3.525}
    for name, (base, spread) in spreads.items():
        noise = np.random.default_rng([zlib.crc32(name.encode()), seed]).standard_normal(out[name].shape)
        drawn = base * np.exp(spread * noise) if base else spread * noise
        out[name] = jnp.asarray(drawn.astype(out[name].dtype))
    for name, factor in factors.items():
        out[name] = (out[name] * factor).astype(out[name].dtype)
    return out
```

```python
from contextlib import ExitStack

import numpy as np
import concourse.bass as bass
from concourse import mybir

F32 = mybir.dt.float32
F32R = mybir.dt.float32r
I32 = mybir.dt.int32
U32 = mybir.dt.uint32
ALU = mybir.AluOpType
ACT = mybir.ActivationFunctionType
AX_X = mybir.AxisListType.X

P = 128
B, S, D, E = 16, 256, 512, 8
TOK = B * S
TOPK = 2
DC = D // P
RC = S // P
TILE = 256
TH = TILE // P
NT = TOK * TOPK // TILE + E - 1
REGION = TOK
NSLOT = E * REGION + NT * TILE
EPS = 1e-5
SCALE = 1.0 / float(np.sqrt(D))


def need(eng, sem, value):
    if not isinstance(value, int) or value > 0:
        eng.wait_ge(sem, value)


def exists(m, count):
    return not isinstance(m, int) or 0 <= m < count


def pipeline(eng, body, first, loop_first, loop_end, end):
    for i in range(first, loop_first):
        body(i)
    with eng.Fori(loop_first, loop_end) as i:
        body(i)
    for i in range(loop_end, end):
        body(i)


BATCHES = (-2, 3, B - 3, B + 2)
TILES = (-4, 2, NT - 4, NT)


def flamingo_block(nc, x, ctx_t, g_xattn, g_ffn, wq_t, wk_t, wv, gate_w, gate_b,
                   w1, w2, w3, b1, b2, b3, out, xn2_dram, slot_tok, slot_w):
    x_v = x.rearrange("b (c p) d -> b p c d", p=P)
    out_v = out.rearrange("b (c p) d -> b p c d", p=P)
    xn2_v = xn2_dram.rearrange("(b c p) d -> b p c d", c=RC, p=P)
    w_dram = [w1, w2, w3]
    b_dram = [b1, b2, b3]

    with ExitStack() as ctx:
        def sem(name):
            return ctx.enter_context(nc.semaphore(name))

        def alloc(stack, name, shape, dt):
            return stack.enter_context(nc.sbuf_tensor(name, shape, dt))

        ident = alloc(ctx, "ident", [P, P], F32)
        tri = alloc(ctx, "tri", [P, P], F32)
        ones = alloc(ctx, "ones", [P, P], F32)
        tg_attn = alloc(ctx, "tg_attn", [P, 1], F32)
        tg_ffn = alloc(ctx, "tg_ffn", [P, 1], F32)
        g_raw = alloc(ctx, "g_raw", [P, 2], F32)
        iota_i = alloc(ctx, "iota_i", [P, E], I32)
        ebase_i = alloc(ctx, "ebase_i", [P, E], I32)
        jidx_i = alloc(ctx, "jidx_i", [P, NT], I32)
        iota_e = alloc(ctx, "iota_e", [P, E], F32)
        ebase = alloc(ctx, "ebase", [P, E], F32)
        jidx = alloc(ctx, "jidx", [P, NT], F32)
        tokall = alloc(ctx, "tokall", [P, B * RC], U32)
        base = alloc(ctx, "base", [P, RC, E], F32)
        table = alloc(ctx, "table", [P, NT, 2], I32)
        tile_onehot = alloc(ctx, "tile_onehot", [P, E, NT], F32)
        vparts = alloc(ctx, "vparts", [P, NT, DC], F32)
        ind16 = alloc(ctx, "ind16", [2 * E, TOK], F32R)

        with ExitStack() as tmp:
            alloc(tmp, "x_head_room", [P, 2 * RC * D], F32)
            wq_raw = alloc(tmp, "wq_raw", [P, DC, D], F32)
            wk_raw = alloc(tmp, "wk_raw", [P, DC, D], F32)
            wv_raw = alloc(tmp, "wv_raw", [P, DC, D], F32)
            wq_hi = alloc(tmp, "wq_hi", [P, DC, D], F32R)
            wq_lo = alloc(tmp, "wq_lo", [P, DC, D], F32R)
            wk_hi = alloc(tmp, "wk_hi", [P, DC, D], F32R)
            wk_lo = alloc(tmp, "wk_lo", [P, DC, D], F32R)
        x_all = alloc(ctx, "x_all", [P, B, RC, D], F32)

        with ExitStack() as ph:
            a_hi = alloc(ph, "a_hi", [P, DC, D], F32R)
            a_lo = alloc(ph, "a_lo", [P, DC, D], F32R)
            wv_hi = alloc(ph, "wv_hi", [P, DC, D], F32R)
            wv_lo = alloc(ph, "wv_lo", [P, DC, D], F32R)
            c_raw = alloc(ph, "c_raw", [P, DC, S], F32)
            c_hi = alloc(ph, "c_hi", [P, DC, S], F32R)
            c_lo = alloc(ph, "c_lo", [P, DC, S], F32R)
            xn = alloc(ph, "xn", [P, RC, D], F32)
            xt_hi = alloc(ph, "xt_hi", [P, DC, S], F32R)
            xt_lo = alloc(ph, "xt_lo", [P, DC, S], F32R)
            qa_hi = alloc(ph, "qa_hi", [P, DC, S], F32R)
            qa_lo = alloc(ph, "qa_lo", [P, DC, S], F32R)
            v_hi = alloc(ph, "v_hi", [P, RC, D], F32R)
            v_lo = alloc(ph, "v_lo", [P, RC, D], F32R)
            pexp = alloc(ph, "pexp", [P, RC, S], F32)
            pt_hi = alloc(ph, "pt_hi", [P, RC, S], F32R)
            pt_lo = alloc(ph, "pt_lo", [P, RC, S], F32R)
            xn2 = alloc(ph, "xn2", [P, RC, D], F32)
            gt_hi = alloc(ph, "gt_hi", [P, DC, S], F32R)
            gt_lo = alloc(ph, "gt_lo", [P, DC, S], F32R)
            gw_raw = alloc(ph, "gw_raw", [P, DC, E], F32)
            gw_hi = alloc(ph, "gw_hi", [P, DC, E], F32R)
            gw_lo = alloc(ph, "gw_lo", [P, DC, E], F32R)
            gb = alloc(ph, "gb", [E, 1], F32)
            st1 = alloc(ph, "st1", [P, RC, 6], F32)
            mv1 = alloc(ph, "mv1", [P, RC, 2], F32)
            rn1 = alloc(ph, "rn1", [P, 4, RC], F32)
            st2 = alloc(ph, "st2", [P, RC, 6], F32)
            mv2 = alloc(ph, "mv2", [P, RC, 2], F32)
            rn2 = alloc(ph, "rn2", [P, 4, RC], F32)
            mhalf = alloc(ph, "mhalf", [P, RC], F32)
            smax = alloc(ph, "smax", [P, RC], F32)
            nbias = alloc(ph, "nbias", [P, RC], F32)
            ssum = alloc(ph, "ssum", [P, RC], F32)
            rsum = alloc(ph, "rsum", [P, RC], F32)
            coef = alloc(ph, "coef", [P, RC], F32)
            logit = alloc(ph, "logit", [E, S], F32)
            gmax = alloc(ph, "gmax", [E, 2], F32)
            gexp = alloc(ph, "gexp", [E, S], F32)
            gsum = alloc(ph, "gsum", [E, 2], F32)
            probs = alloc(ph, "probs", [E, S], F32)
            pr = alloc(ph, "pr", [P, RC, E], F32)
            top = alloc(ph, "top", [P, RC, E], F32)
            topi = alloc(ph, "topi", [P, RC, E], U32)
            topf = alloc(ph, "topf", [P, RC, TOPK], F32)
            oh = alloc(ph, "oh", [P, RC, TOPK, E], F32)
            ind2 = alloc(ph, "ind2", [P, RC, 2, E], F32)
            full = alloc(ph, "full", [P, RC, E], F32)
            prod = alloc(ph, "prod", [P, RC, TOPK, E], F32)
            pos = alloc(ph, "pos", [P, RC, TOPK], F32)
            slot_u = alloc(ph, "slot_u", [P, RC * TOPK], U32)
            tok_u = alloc(ph, "tok_u", [P, RC], U32)
            w_out = alloc(ph, "w_out", [P, RC * TOPK], F32)
            zeros = alloc(ph, "zeros", [P, NSLOT // P], F32)
            cnt = alloc(ph, "cnt", [P, E], F32)
            cnt_i = alloc(ph, "cnt_i", [P, 2, E], I32)
            ntile = alloc(ph, "ntile", [P, E], F32)
            cum = alloc(ph, "cum", [P, E], F32)
            onesE = alloc(ph, "onesE", [P, E], F32)
            le = alloc(ph, "le", [P, NT, E - 1], F32)
            lep = alloc(ph, "lep", [P, NT, E - 1], F32)
            tile_e = alloc(ph, "tile_e", [P, NT], F32)
            tile_prev = alloc(ph, "tile_prev", [P, NT], F32)
            row1 = alloc(ph, "row1", [P, NT], F32)
            row2 = alloc(ph, "row2", [P, NT], F32)
            row3 = alloc(ph, "row3", [P, NT], F32)

        with ExitStack() as ph:
            w_raw = [alloc(ph, f"w_raw{n}", [P, DC, D], F32) for n in range(3)]
            w_hi = [alloc(ph, f"w_hi{n}", [P, DC, D], F32R) for n in range(3)]
            w_lo = [alloc(ph, f"w_lo{n}", [P, DC, D], F32R) for n in range(3)]
            bias = [alloc(ph, f"bias{n}", [P, DC], F32) for n in range(3)]
            idx = alloc(ph, "idx", [P, TH], U32)
            xg = alloc(ph, "xg", [P, TH, D], F32)
            et_hi = alloc(ph, "et_hi", [P, DC, TILE], F32R)
            et_lo = alloc(ph, "et_lo", [P, DC, TILE], F32R)
            h = [alloc(ph, f"h{n}", [P, DC, TILE], F32) for n in range(2)]
            h_hi = [alloc(ph, f"h_hi{n}", [P, DC, TILE], F32R) for n in range(2)]
            h_lo = [alloc(ph, f"h_lo{n}", [P, DC, TILE], F32R) for n in range(2)]
            wb = alloc(ph, "wb", [P, TILE], F32)
            junk = alloc(ph, "junk", [P, TILE], F32)
            nb3 = alloc(ph, "nb3", [P, DC], F32)
            wsum = alloc(ph, "wsum", [P, 1], F32)
            acc = alloc(ph, "acc", [P, DC], F32)
            vprod = alloc(ph, "vprod", [P, E, DC, NT], F32)
            vt = alloc(ph, "vt", [P, E, DC], F32)
            vs = alloc(ph, "vs", [P, E, DC], F32)
            vs_hi = alloc(ph, "vs_hi", [P, E, DC], F32R)
            vhl = alloc(ph, "vhl", [P, DC, 2, E], F32)
            v16 = alloc(ph, "v16", [2 * E, D], F32R)

        bank = [ctx.enter_context(nc.psum_tensor(f"bank{n}", [P, 512], F32)) for n in range(8)]
        bS = bank[0]
        bQ = [bank[1], bank[2]]
        bV = [bank[3], bank[4]]
        bG = [bank[5], bank[6]]
        bR = bank[7]
        bA = [bank[3], bank[4], bank[5], bank[6]]
        bL = [[bank[0], bank[1]], [bank[2], bank[3]], [bank[4], bank[5]]]
        bT = [bank[6], bank[7]]
        R_LOGIT = bR[0:E, 0:S]
        R_IND = bR[0:2 * E, 0:S]
        R_PROB = bR[:, 256:256 + RC * E]
        R_RANK = bR[:, 288:288 + RC * E]
        R_TOT = bR[:, 304:304 + RC * E]

        s_iota = sem("s_iota")
        s_pool_const = sem("s_pool_const")
        s_conv = sem("s_conv")
        s_zero = sem("s_zero")
        s_zero_dma = sem("s_zero_dma")
        s_small = sem("s_small")
        s_tanh = sem("s_tanh")
        s_wqk_in = sem("s_wqk_in")
        s_wv_in = sem("s_wv_in")
        s_wq_hi, s_wk_hi, s_wv_hi, s_gw_hi = sem("s_wq_hi"), sem("s_wk_hi"), sem("s_wv_hi"), sem("s_gw_hi")
        s_wq_lo, s_wk_lo, s_wv_lo, s_gw_lo = sem("s_wq_lo"), sem("s_wk_lo"), sem("s_wv_lo"), sem("s_gw_lo")
        a_mm, a_his, a_los = sem("a_mm"), sem("a_his"), sem("a_los")
        x_in, c_in = sem("x_in"), sem("c_in")
        ln1_stat, ln1_small, xn_ready = sem("ln1_stat"), sem("ln1_small"), sem("xn_ready")
        ln2_stat, ln2_small, xn2_ready = sem("ln2_stat"), sem("ln2_small"), sem("xn2_ready")
        c_his, c_los = sem("c_his"), sem("c_los")
        tx_done, xt_his, xt_los = sem("tx_done"), sem("xt_his"), sem("xt_los")
        qa_done, qa_his, qa_los = sem("qa_done"), sem("qa_his"), sem("qa_los")
        sc_done, nbias_ready, exp_done = sem("sc_done"), sem("nbias_ready"), sem("exp_done")
        tp_done, pt_his, pt_los = sem("tp_done"), sem("pt_his"), sem("pt_los")
        v_done, v_his, v_los = sem("v_done"), sem("v_his"), sem("v_los")
        pv_done, coef_ready, x2_done, xn2_out = sem("pv_done"), sem("coef_ready"), sem("x2_done"), sem("xn2_out")
        tg_done, gt_his, gt_los = sem("tg_done"), sem("gt_his"), sem("gt_los")
        gate_done, gmax_ready, gexp_done, probs_ready = sem("gate_done"), sem("gmax_ready"), sem("gexp_done"), sem("probs_ready")
        pt8_done, top_step, rank_done, slot_step = sem("pt8_done"), sem("top_step"), sem("rank_done"), sem("slot_step")
        scattered = sem("scattered")
        table_step = sem("table_step")
        w_in = [sem(f"w_in{n}") for n in range(3)]
        b_in = [sem(f"b_in{n}") for n in range(3)]
        w_his = [sem(f"w_his{n}") for n in range(3)]
        w_los = [sem(f"w_los{n}") for n in range(3)]
        idx_in, wb_in, gathered = sem("idx_in"), sem("wb_in"), sem("gathered")
        te_done, et_his, et_los = sem("te_done"), sem("et_his"), sem("et_los")
        l_done = [sem(f"l_done{n}") for n in range(3)]
        relu_done = [sem(f"relu_done{n}") for n in range(2)]
        h_his = [sem(f"h_his{n}") for n in range(2)]
        h_los = [sem(f"h_los{n}") for n in range(2)]
        bn_step, gate_step = sem("bn_step"), sem("gate_step")
        tail_small, wsum_step, part_done = sem("tail_small"), sem("wsum_step"), sem("part_done")
        v_step, vt_done, v16_ready = sem("v_step"), sem("vt_done"), sem("v16_ready")
        o_done, res_ready, out_sent = sem("o_done"), sem("res_ready"), sem("out_sent")

        NTOP, NSTEP, NTAB = 9, 9, 14

        waited = {name: sem(f"waited_{name}") for name in ("sp", "pool", "dve", "pe")}

        def wait_alone(eng, name):
            eng.sem_inc(waited[name], 1)

        block = ctx.enter_context(nc.Block())

        @block.sync
        def _(sp):
            sp.dma_start(x_all[:, 0], x_v[0]).then_inc(x_in, 16)
            sp.dma_start(wq_raw[:], wq_t).then_inc(s_wqk_in, 16)
            sp.dma_start(wk_raw[:], wk_t).then_inc(s_wqk_in, 16)
            sp.dma_start(g_raw[:, 0:1], g_xattn.rearrange("(a n) -> a n", a=1).broadcast_to([P, 1])).then_inc(s_small, 16)
            sp.dma_start(g_raw[:, 1:2], g_ffn.rearrange("(a n) -> a n", a=1).broadcast_to([P, 1])).then_inc(s_small, 16)
            sp.dma_start(gw_raw[:], gate_w).then_inc(s_small, 16)
            sp.dma_start(gb[:], gate_b.rearrange("(e n) -> e n", n=1)).then_inc(s_small, 16)
            sp.dma_start(wv_raw[:], wv).then_inc(s_wv_in, 16)
            sp.wait_ge(s_zero, 1)
            sp.dma_start(slot_tok.rearrange("(p n) a -> p (n a)", p=P), zeros[:].bitcast(U32)).then_inc(s_zero_dma, 16)
            sp.dma_start(slot_w.rearrange("(p n) a -> p (n a)", p=P), zeros[:]).then_inc(s_zero_dma, 16)

            def batch(b):
                if exists(b + 1, B):
                    need(sp, c_los, b + 1)
                    sp.dma_start(c_raw[:], ctx_t[b + 1] if isinstance(b, int) else
                                 ctx_t[bass.ds(b + 1, 1)].rearrange("a p c s -> (a p) c s")).then_inc(c_in, 16)
                if exists(b + 3, B):
                    need(sp, x_in, (b + 3) * 16)
                    if isinstance(b, int) and b + 3 == 2:
                        sp.wait_ge(a_mm, DC)
                        sp.wait_ge(s_wv_lo, 1)
                    sp.dma_start(x_all[:, bass.ds(b + 3, 1)], x_v[bass.ds(b + 3, 1)].rearrange("a p c d -> p a c d")
                                 ).then_inc(x_in, 16)
                if exists(b - 1, B):
                    need(sp, xn2_ready, RC * b)
                    sp.dma_start(xn2_v[bass.ds(b - 1, 1)].rearrange("a p c d -> p a c d"),
                                 xn2[:].rearrange("p (a c) d -> p a c d", a=1)).then_inc(xn2_out, 16)

            pipeline(sp, batch, *BATCHES)

            sp.wait_ge(table_step, NTAB)
            sp.wait_ge(scattered, 16 * 8 * B)

            def load_w(n, m):
                need(sp, w_los[n], m)
                wait_alone(sp, "sp")
                e = sp.value_load(table[0:1, bass.ds(m, 1), 0:1], min_val=0, max_val=E - 1)
                sp.dma_start(w_raw[n][:], w_dram[n][bass.ds(e, 1)].rearrange("a p c d -> (a p) c d")
                             ).then_inc(w_in[n], 16)

            def load_b(n, m):
                wait_alone(sp, "sp")
                e = sp.value_load(table[0:1, bass.ds(m, 1), 0:1], min_val=0, max_val=E - 1)
                sp.dma_start(bias[n][:], b_dram[n][bass.ds(e, 1)].rearrange("a p c -> (a p) c")
                             ).then_inc(b_in[n], 16)

            def tile(j):
                if exists(j + 1, NT):
                    load_w(2, j + 1)
                    need(sp, relu_done[1], DC * (j + 1))
                    load_b(1, j + 1)
                if exists(j + 2, NT):
                    load_w(1, j + 2)
                    need(sp, relu_done[0], DC * (j + 2))
                    load_b(0, j + 2)
                if exists(j + 3, NT):
                    load_w(0, j + 3)
                if exists(j + 1, NT):
                    need(sp, part_done, j + 1)
                    load_b(2, j + 1)
                    wait_alone(sp, "sp")
                    r = sp.value_load(table[0:1, bass.ds(j + 1, 1), 1:2], min_val=0, max_val=NSLOT - TILE)
                    sp.dma_start(wb[:], slot_w[bass.ds(r, TILE)].rearrange("n a -> a n").broadcast_to([P, TILE])
                                 ).then_inc(wb_in, 16)
                if exists(j + 4, NT):
                    need(sp, gathered, 16 * TH * (j + 4))
                    wait_alone(sp, "sp")
                    r = sp.value_load(table[0:1, bass.ds(j + 4, 1), 1:2], min_val=0, max_val=NSLOT - TILE)
                    sp.dma_start(idx[:], slot_tok[bass.ds(r, TILE)].rearrange("(p h) a -> p (h a)", p=P)
                                 ).then_inc(idx_in, 16)

            pipeline(sp, tile, *TILES)

            for b in range(B):
                sp.wait_ge(res_ready, RC * (b + 1))
                sp.dma_start(out_v[b], x_all[:, b]).then_inc(out_sent, 16)
            sp.wait_ge(out_sent, 16 * B)

        @block.gpsimd
        def _(pool):
            pool.memset(zeros[:], 0.0).then_inc(s_zero, 1)
            pool.memset(ident[:], 0.0).then_inc(s_iota, 1)
            pool.memset(ones[:], 1.0).then_inc(s_pool_const, 1)
            pool.memset(tri[:], 1.0).then_inc(s_iota, 1)
            pool.memset(mhalf[:], -0.5).then_inc(s_pool_const, 1)
            pool.memset(onesE[:], 1.0).then_inc(s_pool_const, 1)
            pool.wait_ge(s_iota, 2)
            pool.affine_select(out=ident[:], in_=ident[:], compare_op=ALU.not_equal, fill=1.0, base=0,
                               pattern=[[-1, P]], channel_multiplier=1).then_inc(s_pool_const, 1)
            pool.affine_select(out=tri[:], in_=tri[:], compare_op=ALU.is_gt, fill=0.0, base=0,
                               pattern=[[1, P]], channel_multiplier=-1).then_inc(s_pool_const, 1)
            pool.iota(iota_i[:], pattern=[[1, E]], base=0, channel_multiplier=0).then_inc(s_iota, 1)
            pool.iota(ebase_i[:], pattern=[[REGION, E]], base=0, channel_multiplier=0).then_inc(s_iota, 1)
            pool.iota(jidx_i[:], pattern=[[1, NT]], base=0, channel_multiplier=0).then_inc(s_iota, 1)
            pool.iota(tokall[:], pattern=[[P, B * RC]], base=0, channel_multiplier=1).then_inc(s_iota, 1)
            pool.wait_ge(s_pool_const, 5)

            def small_ln(mv, rn, done, m):
                wait_alone(pool, "pool")
                pool.tensor_scalar(rn[:, 0, :], mv[:, :, 1], EPS, None, ALU.add).then_inc(done, 1)
                pool.tensor_scalar(rn[:, 2, :], mv[:, :, 0], -1.0, None, ALU.mult).then_inc(done, 1)
                pool.wait_ge(done, 4 * m + 2)
                pool.tensor_tensor(rn[:, 1, :], rn[:, 0, :], mhalf[:], ALU.pow).then_inc(done, 1)
                pool.wait_ge(done, 4 * m + 3)
                pool.tensor_tensor(rn[:, 3, :], rn[:, 2, :], rn[:, 1, :], ALU.mult).then_inc(done, 1)

            def batch(b):
                if exists(b + 2, B):
                    need(pool, ln1_stat, RC * (b + 3))
                    need(pool, xn_ready, RC * (b + 2))
                    small_ln(mv1, rn1, ln1_small, b + 2)
                if exists(b - 2, B):
                    need(pool, slot_step, NSTEP * (b - 1))
                    if isinstance(b, int) and b == 2:
                        pool.wait_ge(s_zero_dma, 32)
                    wait_alone(pool, "pool")
                    for n in range(RC * TOPK):
                        where = bass.IndirectOffsetOnAxis(ap=slot_u[:, n:n + 1], axis=0)
                        pool.indirect_dma_start(slot_tok, where, tok_u[:, n // TOPK:n // TOPK + 1], None
                                                ).then_inc(scattered, 16)
                        pool.indirect_dma_start(slot_w, where, w_out[:, n:n + 1], None).then_inc(scattered, 16)
                if exists(b + 1, B):
                    need(pool, c_his, b + 2)
                    pool.tensor_tensor(c_lo[:], c_raw[:], c_hi[:].bitcast(F32), ALU.subtract).then_inc(c_los, 1)
                if exists(b, B):
                    need(pool, ln2_stat, RC * (b + 1))
                    need(pool, xn2_ready, RC * b)
                    small_ln(mv2, rn2, ln2_small, b)

            pipeline(pool, batch, *BATCHES)

            pool.wait_ge(xn2_out, 16 * B)

            def tile(j):
                if exists(j, NT):
                    for k in range(2):
                        pool.wait_ge(h_his[1], 2 * j + k + 1)
                        pool.tensor_tensor(h_lo[1][:, 2 * k:2 * k + 2], h[1][:, 2 * k:2 * k + 2],
                                           h_hi[1][:, 2 * k:2 * k + 2].bitcast(F32), ALU.subtract).then_inc(h_los[1], 1)
                if exists(j + 1, NT):
                    for k in range(2):
                        pool.wait_ge(h_his[0], 2 * (j + 1) + k + 1)
                        pool.tensor_tensor(h_lo[0][:, 2 * k:2 * k + 2], h[0][:, 2 * k:2 * k + 2],
                                           h_hi[0][:, 2 * k:2 * k + 2].bitcast(F32), ALU.subtract).then_inc(h_los[0], 1)
                if exists(j + 3, NT):
                    need(pool, idx_in, 16 * (j + 4))
                    need(pool, te_done, 2 * (j + 3))
                    wait_alone(pool, "pool")
                    for t in range(TH):
                        pool.indirect_dma_start(xg[:, t], None, xn2_dram,
                                                bass.IndirectOffsetOnAxis(ap=idx[:, t:t + 1], axis=0)
                                                ).then_inc(gathered, 16)

            pipeline(pool, tile, *TILES)

        @block.scalar
        def _(act):
            act.wait_ge(s_small, 64)
            act.activation(tg_attn[:], g_raw[:, 0:1], ACT.Tanh).then_inc(s_tanh, 1)
            act.activation(tg_ffn[:], g_raw[:, 1:2], ACT.Tanh).then_inc(s_tanh, 1)
            act.activation(gw_hi[:], gw_raw[:], ACT.Copy).then_inc(s_gw_hi, 1)

            def batch(b):
                if exists(b, B):
                    need(act, nbias_ready, 2 * (b + 1))
                    need(act, tp_done, b)
                    for c in range(RC):
                        act.activation(pexp[:, c], bS[:, c * S:(c + 1) * S], ACT.Exp, bias=nbias[:, c:c + 1],
                                       scale=SCALE, accum_out=ssum[:, c:c + 1]).then_inc(exp_done, 1)
                if exists(b + 1, B):
                    for k in range(2):
                        need(act, tx_done, 2 * (b + 1) + k + 1)
                        need(act, qa_done, 2 * (b + 1))
                        act.activation(xt_hi[:, 2 * k:2 * k + 2], bQ[k][:].rearrange("p (c s) -> p c s", c=2),
                                       ACT.Copy).then_inc(xt_his, 1)
                if exists(b + 2, B):
                    need(act, ln1_small, 4 * (b + 3))
                    need(act, tx_done, 2 * (b + 2))
                    for c in range(RC):
                        act.activation(xn[:, c], x_all[:, bass.ds(b + 2, 1), c].rearrange("p a d -> p (a d)"),
                                       ACT.Identity, bias=rn1[:, 3, c:c + 1], scale=rn1[:, 1, c:c + 1]
                                       ).then_inc(xn_ready, 1)
                if exists(b, B):
                    need(act, pv_done, 2 * b)
                    for k in range(RC):
                        need(act, v_done, 2 * b + k + 1)
                        act.activation(v_hi[:, k], bV[k][:], ACT.Copy).then_inc(v_his, 1)
                    need(act, tp_done, b + 1)
                    act.activation(pt_hi[:], bS[:].rearrange("p (c s) -> p c s", c=RC), ACT.Copy).then_inc(pt_his, 1)
                if exists(b - 1, B):
                    need(act, gate_done, b - 1)
                    for k in range(2):
                        need(act, tg_done, 2 * (b - 1) + k + 1)
                        act.activation(gt_hi[:, 2 * k:2 * k + 2], bG[k][:].rearrange("p (c s) -> p c s", c=2),
                                       ACT.Copy).then_inc(gt_his, 1)
                if exists(b + 1, B):
                    need(act, c_in, 16 * (b + 2))
                    need(act, v_done, 2 * (b + 1))
                    act.activation(c_hi[:], c_raw[:], ACT.Copy).then_inc(c_his, 1)
                    need(act, sc_done, b + 1)
                    for k in range(2):
                        need(act, qa_done, 2 * (b + 1) + k + 1)
                        act.activation(qa_hi[:, 2 * k:2 * k + 2], bQ[k][:].rearrange("p (c s) -> p c s", c=2),
                                       ACT.Copy).then_inc(qa_his, 1)
                if exists(b - 1, B):
                    need(act, gmax_ready, 2 * b)
                    act.activation(gexp[:], logit[:], ACT.Exp, bias=gmax[:, 1:2], accum_out=gsum[:, 0:1]
                                   ).then_inc(gexp_done, 1)
                if exists(b, B):
                    need(act, ln2_small, 4 * (b + 1))
                    need(act, tg_done, 2 * b)
                    need(act, xn2_out, 16 * b)
                    for c in range(RC):
                        act.activation(xn2[:, c], x_all[:, bass.ds(b, 1), c].rearrange("p a d -> p (a d)"),
                                       ACT.Identity, bias=rn2[:, 3, c:c + 1], scale=rn2[:, 1, c:c + 1]
                                       ).then_inc(xn2_ready, 1)

            batch(-2)
            act.wait_ge(s_wqk_in, 32)
            act.activation(wq_hi[:], wq_raw[:], ACT.Copy).then_inc(s_wq_hi, 1)
            act.wait_ge(s_wv_in, 16)
            act.activation(wv_hi[:], wv_raw[:], ACT.Copy).then_inc(s_wv_hi, 1)
            for n in range(DC):
                act.wait_ge(a_mm, n + 1)
                act.activation(a_hi[:, n], bA[n][:], ACT.Copy).then_inc(a_his, 1)
            pipeline(act, batch, -1, *BATCHES[1:])

            def split_w(n, m):
                act.wait_ge(w_in[n], 16 * (m + 1))
                need(act, l_done[n], 2 * m)
                act.activation(w_hi[n][:], w_raw[n][:], ACT.Copy).then_inc(w_his[n], 1)

            def relu(n, m):
                act.wait_ge(b_in[n], 16 * (m + 1))
                for oc in range(DC):
                    if oc % 2 == 0:
                        act.wait_ge(l_done[n], 2 * m + oc // 2 + 1)
                        need(act, h_los[n], 2 * (m - 1) + oc // 2 + 1)
                    act.activation(h[n][:, oc], bL[n][oc // 2][:, (oc % 2) * TILE:(oc % 2 + 1) * TILE], ACT.Relu,
                                   bias=bias[n][:, oc:oc + 1]).then_inc(relu_done[n], 1)

            def tile(j):
                if exists(j, NT):
                    split_w(2, j)
                    relu(1, j)
                if exists(j + 1, NT):
                    split_w(1, j + 1)
                    relu(0, j + 1)
                if exists(j + 2, NT):
                    split_w(0, j + 2)
                    need(act, l_done[0], 2 * (j + 2))
                    for k in range(2):
                        act.wait_ge(te_done, 2 * (j + 2) + k + 1)
                        act.activation(et_hi[:, 2 * k:2 * k + 2], bT[k][:].rearrange("p (c s) -> p c s", c=2),
                                       ACT.Copy).then_inc(et_his, 1)

            pipeline(act, tile, *TILES)

        @block.vector
        def _(dve):
            dve.wait_ge(s_iota, 6)
            dve.tensor_copy(iota_e[:], iota_i[:]).then_inc(s_conv, 1)
            dve.tensor_copy(ebase[:], ebase_i[:]).then_inc(s_conv, 1)
            dve.tensor_copy(jidx[:], jidx_i[:]).then_inc(s_conv, 1)
            dve.tensor_copy(base[:, 0], ebase_i[:]).then_inc(s_conv, 1)
            dve.wait_ge(s_conv, 4)

            def stats(src_batch, st, mv, done, step_sem_base):
                wait_alone(dve, "dve")
                for c in range(RC):
                    dve.bn_stats(st[:, c], x_all[:, bass.ds(src_batch, 1), c].rearrange("p a d -> p (a d)")
                                 ).then_inc(bn_step, 1)
                dve.wait_ge(bn_step, step_sem_base + RC)
                wait_alone(dve, "dve")
                for c in range(RC):
                    dve.bn_aggr(mv[:, c], st[:, c]).then_inc(done, 1)

            def low(dst, src, hi, done):
                dve.tensor_tensor(dst, src, hi.bitcast(F32), ALU.subtract).then_inc(done, 1)

            def two(bk):
                return bk[:].rearrange("p (c s) -> p c s", c=2)

            def batch(b):
                if exists(b, B):
                    need(dve, sc_done, b + 1)
                    dve.tensor_reduce(smax[:], bS[:].rearrange("p (c s) -> p c s", c=RC), AX_X, ALU.max
                                      ).then_inc(nbias_ready, 1)
                    dve.wait_ge(nbias_ready, 2 * b + 1)
                    dve.tensor_scalar(nbias[:], smax[:], -SCALE, None, ALU.mult).then_inc(nbias_ready, 1)
                if exists(b + 2, B):
                    need(dve, x_in, 16 * (b + 3))
                    need(dve, ln1_small, 4 * (b + 2))
                    stats(b + 2, st1, mv1, ln1_stat, bn_before(b + 2, True))
                if exists(b + 1, B):
                    for k in range(2):
                        need(dve, xt_his, 2 * (b + 1) + k + 1)
                        low(xt_lo[:, 2 * k:2 * k + 2], two(bQ[k]), xt_hi[:, 2 * k:2 * k + 2], xt_los)
                if exists(b - 2, B):
                    m = b - 2
                    need(dve, rank_done, m + 1)
                    dve.tensor_copy(ind16[:, bass.ds(m * S, S)], R_IND).then_inc(slot_step, 1)
                    dve.tensor_tensor(base[:, 1], base[:, 0], R_TOT[:, 0:E], ALU.add).then_inc(slot_step, 1)
                    dve.wait_ge(slot_step, NSTEP * m + 2)
                    dve.tensor_tensor(full[:].rearrange("p c e -> p (c e)"), R_RANK,
                                      base[:].rearrange("p c e -> p (c e)"), ALU.add).then_inc(slot_step, 1)
                    dve.wait_ge(slot_step, NSTEP * m + 3)
                    dve.tensor_tensor(base[:, 0], base[:, 1], R_TOT[:, E:2 * E], ALU.add).then_inc(slot_step, 1)
                    dve.tensor_tensor(prod[:], oh[:], full[:].unsqueeze(2).broadcast_to([P, RC, TOPK, E]), ALU.mult
                                      ).then_inc(slot_step, 1)
                    dve.wait_ge(slot_step, NSTEP * m + 5)
                    dve.tensor_reduce(pos[:], prod[:], AX_X, ALU.add).then_inc(slot_step, 1)
                    dve.wait_ge(slot_step, NSTEP * m + 6)
                    need(dve, scattered, 128 * m)
                    dve.tensor_copy(slot_u[:], pos[:].rearrange("p c k -> p (c k)")).then_inc(slot_step, 1)
                    dve.tensor_copy(tok_u[:], tokall[:, bass.ds(m * RC, RC)]).then_inc(slot_step, 1)
                    dve.tensor_copy(w_out[:].rearrange("p (c k) -> p c k", c=RC), top[:, :, 0:TOPK]
                                    ).then_inc(slot_step, 1)
                if exists(b, B):
                    for k in range(RC):
                        need(dve, v_his, 2 * b + k + 1)
                        low(v_lo[:, k], bV[k][:], v_hi[:, k], v_los)
                    need(dve, pt_his, b + 1)
                    low(pt_lo[:], two(bS), pt_hi[:], pt_los)
                if exists(b - 1, B):
                    for k in range(2):
                        need(dve, gt_his, 2 * (b - 1) + k + 1)
                        low(gt_lo[:, 2 * k:2 * k + 2], two(bG[k]), gt_hi[:, 2 * k:2 * k + 2], gt_los)
                if exists(b + 1, B):
                    for k in range(2):
                        need(dve, qa_his, 2 * (b + 1) + k + 1)
                        low(qa_lo[:, 2 * k:2 * k + 2], two(bQ[k]), qa_hi[:, 2 * k:2 * k + 2], qa_los)
                if exists(b - 1, B):
                    m = b - 1
                    need(dve, gate_done, m + 1)
                    dve.tensor_scalar(logit[:], R_LOGIT, gb[:, 0:1], None, ALU.add).then_inc(gate_step, 1)
                    dve.wait_ge(gate_step, 2 * m + 1)
                    dve.tensor_reduce(gmax[:, 0:1], logit[:], AX_X, ALU.max).then_inc(gmax_ready, 1)
                    dve.wait_ge(gmax_ready, 2 * m + 1)
                    dve.tensor_scalar(gmax[:, 1:2], gmax[:, 0:1], -1.0, None, ALU.mult).then_inc(gmax_ready, 1)
                    dve.wait_ge(gexp_done, m + 1)
                    dve.reciprocal(gsum[:, 1:2], gsum[:, 0:1]).then_inc(gate_step, 1)
                    dve.wait_ge(gate_step, 2 * m + 2)
                    dve.tensor_scalar(probs[:], gexp[:], gsum[:, 1:2], None, ALU.mult).then_inc(probs_ready, 1)
                if exists(b, B):
                    need(dve, exp_done, RC * (b + 1))
                    dve.reciprocal(rsum[:], ssum[:]).then_inc(coef_ready, 1)
                    dve.wait_ge(coef_ready, 2 * b + 1)
                    dve.tensor_scalar(coef[:], rsum[:], tg_attn[:, 0:1], None, ALU.mult).then_inc(coef_ready, 1)
                    dve.wait_ge(coef_ready, 2 * b + 2)
                    for c in range(RC):
                        row = x_all[:, bass.ds(b, 1), c].rearrange("p a d -> p (a d)")
                        need(dve, pv_done, 2 * b + c + 1)
                        dve.scalar_tensor_tensor(out=row, in0=bV[c][:], scalar=coef[:, c:c + 1], in1=row,
                                                 op0=ALU.mult, op1=ALU.add).then_inc(x2_done, 1)
                    dve.wait_ge(x2_done, 2 * b + 2)
                    need(dve, ln2_small, 4 * b)
                    stats(b, st2, mv2, ln2_stat, bn_before(b, False))
                if exists(b - 1, B):
                    m = b - 1
                    need(dve, pt8_done, m + 1)
                    dve.tensor_copy(pr[:].rearrange("p c e -> p (c e)"), R_PROB).then_inc(top_step, 1)
                    dve.wait_ge(top_step, NTOP * m + 1)
                    wait_alone(dve, "dve")
                    for c in range(RC):
                        dve.max(top[:, c], pr[:, c]).then_inc(top_step, 1)
                    dve.wait_ge(top_step, NTOP * m + 3)
                    wait_alone(dve, "dve")
                    for c in range(RC):
                        dve.max_index(topi[:, c], top[:, c], pr[:, c]).then_inc(top_step, 1)
                    dve.wait_ge(top_step, NTOP * m + 5)
                    dve.tensor_copy(topf[:], topi[:, :, 0:TOPK]).then_inc(top_step, 1)
                    dve.wait_ge(top_step, NTOP * m + 6)
                    dve.tensor_tensor(oh[:].rearrange("p c k e -> p (c k) e"),
                                      topf[:].rearrange("p c k -> p (c k)").unsqueeze(2).broadcast_to([P, RC * TOPK, E]),
                                      iota_e[:].unsqueeze(1).broadcast_to([P, RC * TOPK, E]), ALU.is_equal
                                      ).then_inc(top_step, 1)
                    dve.wait_ge(top_step, NTOP * m + 7)
                    for r in range(2):
                        dve.tensor_tensor(ind2[:, :, r], oh[:, :, 0], oh[:, :, 1], ALU.add).then_inc(top_step, 1)

            def bn_before(m, first_norm):
                if first_norm:
                    seconds = m - 2 if not isinstance(m, int) else max(0, m - 2)
                    return RC * (m + seconds)
                firsts = m + 3 if not isinstance(m, int) else min(B, m + 3)
                return RC * (m + firsts)

            batch(-2)
            dve.wait_ge(s_wqk_in, 32)
            dve.tensor_copy(wk_hi[:], wk_raw[:]).then_inc(s_wk_hi, 1)
            dve.wait_ge(s_wq_hi, 1)
            low(wq_lo[:], wq_raw[:], wq_hi[:], s_wq_lo)
            dve.wait_ge(s_wk_hi, 1)
            low(wk_lo[:], wk_raw[:], wk_hi[:], s_wk_lo)
            dve.wait_ge(s_gw_hi, 1)
            low(gw_lo[:], gw_raw[:], gw_hi[:], s_gw_lo)
            dve.wait_ge(s_wv_hi, 1)
            low(wv_lo[:], wv_raw[:], wv_hi[:], s_wv_lo)
            for n in range(DC):
                dve.wait_ge(a_his, n + 1)
                low(a_lo[:, n], bA[n][:], a_hi[:, n], a_los)
            dve.wait_ge(s_tanh, 2)
            pipeline(dve, batch, -1, *BATCHES[1:])

            step = [0]

            def link(ins):
                step[0] += 1
                ins.then_inc(table_step, 1)
                dve.wait_ge(table_step, step[0])

            dve.wait_ge(slot_step, NSTEP * B)
            link(dve.tensor_tensor(cnt[:], base[:, 0], ebase[:], ALU.subtract))
            link(dve.tensor_scalar(cnt_i[:, 0], cnt[:], float(TILE - 1), None, ALU.add))
            link(dve.tensor_scalar(cnt_i[:, 1], cnt_i[:, 0], 8, None, ALU.arith_shift_right))
            link(dve.tensor_copy(ntile[:], cnt_i[:, 1]))
            link(dve.tensor_tensor_scan(cum[:], onesE[:], ntile[:], 0.0, ALU.mult, ALU.add))
            link(dve.tensor_tensor(le[:], cum[:, 0:E - 1].unsqueeze(1).broadcast_to([P, NT, E - 1]),
                                   jidx[:].unsqueeze(2).broadcast_to([P, NT, E - 1]), ALU.is_le))
            link(dve.tensor_reduce(tile_e[:], le[:], AX_X, ALU.add))
            link(dve.tensor_tensor(lep[:], le[:], ntile[:, 0:E - 1].unsqueeze(1).broadcast_to([P, NT, E - 1]), ALU.mult))
            link(dve.tensor_reduce(tile_prev[:], lep[:], AX_X, ALU.add))
            link(dve.tensor_tensor(row1[:], jidx[:], tile_prev[:], ALU.subtract))
            link(dve.tensor_scalar(row2[:], row1[:], float(TILE), None, ALU.mult))
            link(dve.scalar_tensor_tensor(out=row3[:], in0=tile_e[:], scalar=float(REGION), in1=row2[:],
                                          op0=ALU.mult, op1=ALU.add))
            link(dve.tensor_copy(table[:, :, 0], tile_e[:]))
            link(dve.tensor_copy(table[:, :, 1], row3[:]))
            dve.tensor_tensor(tile_onehot[:], tile_e[:].unsqueeze(1).broadcast_to([P, E, NT]),
                              iota_e[:].unsqueeze(2).broadcast_to([P, E, NT]), ALU.is_equal).then_inc(v_step, 1)

            def split_w(n, m):
                dve.wait_ge(w_his[n], m + 1)
                low(w_lo[n][:], w_raw[n][:], w_hi[n][:], w_los[n])

            def h_high(n, m):
                need(dve, l_done[n + 1], 2 * m)
                for k in range(2):
                    dve.wait_ge(relu_done[n], DC * m + 2 * k + 2)
                    dve.tensor_copy(h_hi[n][:, 2 * k:2 * k + 2], h[n][:, 2 * k:2 * k + 2]).then_inc(h_his[n], 1)

            def tile(j):
                if exists(j, NT):
                    split_w(2, j)
                    h_high(1, j)
                if exists(j + 1, NT):
                    split_w(1, j + 1)
                    h_high(0, j + 1)
                if exists(j + 2, NT):
                    split_w(0, j + 2)
                    for k in range(2):
                        dve.wait_ge(et_his, 2 * (j + 2) + k + 1)
                        low(et_lo[:, 2 * k:2 * k + 2], two(bT[k]), et_hi[:, 2 * k:2 * k + 2], et_los)
                if exists(j, NT):
                    dve.wait_ge(b_in[2], 16 * (j + 1))
                    dve.wait_ge(wb_in, 16 * (j + 1))
                    dve.tensor_scalar(nb3[:], bias[2][:], -1.0, None, ALU.mult).then_inc(wsum_step, 1)
                    dve.tensor_reduce(wsum[:], wb[:], AX_X, ALU.add).then_inc(wsum_step, 1)
                    dve.wait_ge(wsum_step, 2 * j + 2)
                    for oc in range(DC):
                        if oc % 2 == 0:
                            dve.wait_ge(l_done[2], 2 * j + oc // 2 + 1)
                        z = bL[2][oc // 2][:, (oc % 2) * TILE:(oc % 2 + 1) * TILE]
                        dve.scalar_tensor_tensor(out=junk[:].rearrange("p (h t) -> p h t", h=TH),
                                                 in0=z.rearrange("p (h t) -> p h t", h=TH), scalar=nb3[:, oc:oc + 1],
                                                 in1=wb[:].rearrange("p (t h) -> p h t", h=TH),
                                                 op0=ALU.max, op1=ALU.mult,
                                                 accum_out=acc[:, oc:oc + 1]).then_inc(tail_small, 1)
                        dve.wait_ge(tail_small, DC * j + oc + 1)
                    dve.scalar_tensor_tensor(out=vparts[:, bass.ds(j, 1)].rearrange("p a c -> p (a c)"),
                                             in0=bias[2][:], scalar=wsum[:, 0:1], in1=acc[:],
                                             op0=ALU.mult, op1=ALU.add).then_inc(part_done, 1)

            pipeline(dve, tile, *TILES)

            vstep = [1]

            def vlink(ins):
                vstep[0] += 1
                ins.then_inc(v_step, 1)
                dve.wait_ge(v_step, vstep[0])

            dve.wait_ge(part_done, NT)
            dve.wait_ge(v_step, 1)
            for e in range(E):
                last = dve.tensor_tensor(vprod[:, e], vparts[:].rearrange("p j c -> p c j"),
                                         tile_onehot[:, e].unsqueeze(1).broadcast_to([P, DC, NT]), ALU.mult)
                vlink(last)
            vlink(dve.tensor_reduce(vt[:], vprod[:], AX_X, ALU.add))
            vlink(dve.tensor_scalar(vs[:], vt[:], tg_ffn[:, 0:1], None, ALU.mult))
            vlink(dve.tensor_copy(vs_hi[:], vs[:]))
            vlink(dve.tensor_copy(vhl[:, :, 0], vs_hi[:].bitcast(F32).rearrange("p e c -> p c e")))
            vlink(dve.tensor_tensor(vhl[:, :, 1], vs[:].rearrange("p e c -> p c e"),
                                    vs_hi[:].bitcast(F32).rearrange("p e c -> p c e"), ALU.subtract))
            dve.wait_ge(vt_done, 1)
            dve.tensor_copy(v16[:], bank[0][0:2 * E, :]).then_inc(v16_ready, 1)

            for n in range(B * RC):
                dve.wait_ge(o_done, n + 1)
                row = x_all[:, n // RC, n % RC]
                dve.tensor_tensor(row, bank[n % 8][:], row, ALU.add).then_inc(res_ready, 1)

        @block.tensor
        def _(pe):
            def split_product(out_ap, left, right, done=None):
                n = len(left[0])
                for i in range(n):
                    lh, ll, rh, rl = left[0][i], left[1][i], right[0][i], right[1][i]
                    pe.matmul(out_ap, lh, rh, start=(i == 0), stop=False)
                    pe.matmul(out_ap, lh, rl, start=False, stop=False)
                    last = pe.matmul(out_ap, ll, rh, start=False, stop=(i == n - 1))
                if done is not None:
                    last.then_inc(done, 1)

            def cols(hi, lo, a, width):
                return ([hi[:, c, a:a + width] for c in range(hi.shape[1])],
                        [lo[:, c, a:a + width] for c in range(lo.shape[1])])

            def transpose_rows(src, banks, done):
                for dc in range(DC):
                    for c in range(RC):
                        last = pe.transpose(banks[dc // 2][:, (dc % 2) * S + c * P:(dc % 2) * S + (c + 1) * P],
                                            src[:, c, dc * P:(dc + 1) * P], ident[:])
                    if dc % 2 == 1:
                        last.then_inc(done, 1)

            pe.wait_ge(s_wq_lo, 1)
            pe.wait_ge(s_wk_lo, 1)
            for n in range(DC):
                split_product(bA[n][:], cols(wq_hi, wq_lo, n * P, P), cols(wk_hi, wk_lo, 0, D), a_mm)
            pe.wait_ge(s_pool_const, 5)
            pe.wait_ge(s_wv_lo, 1)
            pe.wait_ge(s_gw_lo, 1)
            pe.wait_ge(a_los, DC)

            def batch(b):
                if exists(b, B):
                    need(pe, qa_los, 2 * (b + 1))
                    need(pe, c_los, b + 1)
                    need(pe, pt_los, b)
                    for c in range(RC):
                        split_product(bS[:, c * S:(c + 1) * S], cols(qa_hi, qa_lo, c * P, P), cols(c_hi, c_lo, 0, S),
                                      sc_done if c == RC - 1 else None)
                if exists(b + 1, B):
                    need(pe, xn_ready, RC * (b + 2))
                    need(pe, qa_los, 2 * (b + 1))
                    transpose_rows(xn, bQ, tx_done)
                if exists(b - 2, B):
                    need(pe, top_step, NTOP * (b - 1))
                    ind = ind2[:, :, 0]
                    pe.matmul(R_RANK, tri[:], ind, start=True, stop=True)
                    pe.matmul(R_TOT, ones[:], ind, start=True, stop=True)
                    for c in range(RC):
                        last = pe.transpose(bR[0:2 * E, c * P:(c + 1) * P],
                                            ind2[:, c].rearrange("p r e -> p (r e)"), ident[:])
                    last.then_inc(rank_done, 1)
                if exists(b, B):
                    need(pe, x2_done, 2 * b)
                    for c in range(RC):
                        split_product(bV[c][:], cols(c_hi, c_lo, c * P, P), cols(wv_hi, wv_lo, 0, D), v_done)
                    need(pe, exp_done, RC * (b + 1))
                    for k in range(RC):
                        for c in range(RC):
                            last = pe.transpose(bS[:, k * S + c * P:k * S + (c + 1) * P],
                                                pexp[:, c, k * P:(k + 1) * P], ident[:])
                    last.then_inc(tp_done, 1)
                if exists(b - 1, B):
                    need(pe, xn2_ready, RC * b)
                    need(pe, gt_los, 2 * (b - 1))
                    transpose_rows(xn2, bG, tg_done)
                if exists(b + 1, B):
                    need(pe, xt_los, 2 * (b + 2))
                    for n in range(DC):
                        split_product(bQ[n // 2][:, (n % 2) * S:(n % 2 + 1) * S], cols(a_hi, a_lo, n * P, P),
                                      cols(xt_hi, xt_lo, 0, S), qa_done if n % 2 == 1 else None)
                if exists(b - 1, B):
                    need(pe, gt_los, 2 * b)
                    need(pe, slot_step, NSTEP * (b - 2) + 4)
                    split_product(R_LOGIT, cols(gw_hi, gw_lo, 0, E), cols(gt_hi, gt_lo, 0, S), gate_done)
                if exists(b, B):
                    need(pe, pt_los, b + 1)
                    need(pe, v_los, 2 * (b + 1))
                    for c in range(RC):
                        split_product(bV[c][:], cols(pt_hi, pt_lo, c * P, P), cols(v_hi, v_lo, 0, D), pv_done)
                if exists(b - 1, B):
                    need(pe, probs_ready, b)
                    wait_alone(pe, "pe")
                    for c in range(RC):
                        last = pe.transpose(R_PROB[:, c * E:(c + 1) * E], probs[:, c * P:(c + 1) * P],
                                            ident[0:E, 0:E])
                    last.then_inc(pt8_done, 1)

            pipeline(pe, batch, *BATCHES)

            def layer(n, m, src_hi, src_lo):
                for oc in range(DC):
                    split_product(bL[n][oc // 2][:, (oc % 2) * TILE:(oc % 2 + 1) * TILE],
                                  cols(w_hi[n], w_lo[n], oc * P, P), cols(src_hi, src_lo, 0, TILE),
                                  l_done[n] if oc % 2 == 1 else None)

            def tile(j):
                if exists(j, NT):
                    need(pe, w_los[1], j + 1)
                    need(pe, h_los[0], 2 * (j + 1))
                    need(pe, relu_done[1], DC * j)
                    layer(1, j, h_hi[0], h_lo[0])
                if exists(j + 1, NT):
                    need(pe, w_los[0], j + 2)
                    need(pe, et_los, 2 * (j + 2))
                    need(pe, relu_done[0], DC * (j + 1))
                    layer(0, j + 1, et_hi, et_lo)
                if exists(j + 2, NT):
                    need(pe, gathered, 16 * TH * (j + 3))
                    need(pe, et_los, 2 * (j + 2))
                    transpose_rows(xg, bT, te_done)
                if exists(j, NT):
                    need(pe, w_los[2], j + 1)
                    need(pe, h_los[1], 2 * (j + 1))
                    need(pe, part_done, j)
                    layer(2, j, h_hi[1], h_lo[1])

            pipeline(pe, tile, *TILES)

            pe.wait_ge(v_step, 1 + E + 5)
            for c in range(DC):
                last = pe.transpose(bank[0][0:2 * E, c * P:(c + 1) * P],
                                    vhl[:, c].rearrange("p r e -> p (r e)"), ident[:])
            last.then_inc(vt_done, 1)
            pe.wait_ge(v16_ready, 1)
            for n in range(B * RC):
                need(pe, res_ready, n - 7)
                pe.matmul(bank[n % 8][:], ind16[:, n * P:(n + 1) * P], v16[:], start=True, stop=True
                          ).then_inc(o_done, 1)


def _chunks(a):
    lead = a.shape[:-2]
    a = a.reshape(*lead, a.shape[-2] // P, P, a.shape[-1])
    return np.ascontiguousarray(np.swapaxes(a, -3, -2))


def kernel(x, ctx_1024, g_xattn, g_ffn, L0_xattn_Wq, L0_xattn_Wkv, L0_ffn_gate_w, L0_ffn_gate_b,
           L0_ffn_w1, L0_ffn_b1, L0_ffn_w2, L0_ffn_b2, L0_ffn_w3, L0_ffn_b3):
    import concourse.bacc as _bacc
    from concourse.bass_utils import run_bass_kernel_spmd as _run

    wkv = np.asarray(L0_xattn_Wkv)
    arrays = {
        "x": np.ascontiguousarray(x),
        "ctx_t": _chunks(np.swapaxes(np.asarray(ctx_1024), 1, 2)),
        "g_xattn": np.ascontiguousarray(g_xattn),
        "g_ffn": np.ascontiguousarray(g_ffn),
        "wq_t": _chunks(np.asarray(L0_xattn_Wq).T),
        "wk_t": _chunks(wkv[:, :D].T),
        "wv": _chunks(wkv[:, D:]),
        "gate_w": _chunks(np.asarray(L0_ffn_gate_w)),
        "gate_b": np.ascontiguousarray(L0_ffn_gate_b),
        "w1": _chunks(np.asarray(L0_ffn_w1)),
        "w2": _chunks(np.asarray(L0_ffn_w2)),
        "w3": _chunks(np.asarray(L0_ffn_w3)),
        "b1": np.ascontiguousarray(np.swapaxes(np.asarray(L0_ffn_b1).reshape(E, DC, P), 1, 2)),
        "b2": np.ascontiguousarray(np.swapaxes(np.asarray(L0_ffn_b2).reshape(E, DC, P), 1, 2)),
        "b3": np.ascontiguousarray(np.swapaxes(np.asarray(L0_ffn_b3).reshape(E, DC, P), 1, 2)),
    }
    nc = _bacc.Bacc("TRN2", target_bir_lowering=False, num_devices=1)
    args = [nc.dram_tensor(f"in_{k}", a.shape, F32, kind="ExternalInput").ap() for k, a in arrays.items()]
    out = nc.dram_tensor("out", (B, S, D), F32, kind="ExternalOutput").ap()
    xn2_dram = nc.dram_tensor("xn2_dram", (TOK, D), F32).ap()
    slot_tok = nc.dram_tensor("slot_tok", (NSLOT, 1), U32).ap()
    slot_w = nc.dram_tensor("slot_w", (NSLOT, 1), F32).ap()
    flamingo_block(nc, *args, out, xn2_dram, slot_tok, slot_w)
    r = _run(nc, [{f"in_{k}": a for k, a in arrays.items()}], core_ids=[0])
    return r.results[0]["out"]
```

```python
from contextlib import ExitStack

import numpy as np
import concourse.bass as bass
from concourse import mybir

F32 = mybir.dt.float32
F32R = mybir.dt.float32r
I32 = mybir.dt.int32
U32 = mybir.dt.uint32
ALU = mybir.AluOpType
ACT = mybir.ActivationFunctionType
AX_X = mybir.AxisListType.X

P = 128
B, S, D, E = 16, 256, 512, 8
TOK = B * S
TOPK = 2
DC = D // P
RC = S // P
TILE = 256
TH = TILE // P
NT_MIN = TOK * TOPK // TILE
NT = NT_MIN + E - 1
REGION = TOK
NSLOT = E * REGION
EPS = 1e-5
SCALE = 1.0 / float(np.sqrt(D))


def need(eng, sem, value):
    if not isinstance(value, int) or value > 0:
        eng.wait_ge(sem, value)


def exists(m, count):
    return not isinstance(m, int) or 0 <= m < count


def pipeline(eng, body, first, loop_first, loop_end, end):
    for i in range(first, loop_first):
        body(i)
    with eng.Fori(loop_first, loop_end) as i:
        body(i)
    for i in range(loop_end, end):
        body(i)


BATCHES = (-1, 3, B - 3, B + 2)

AHEAD = 4


def tile_pipeline(eng, body, tiles):
    for j in range(-AHEAD, 2):
        body(j, AHEAD + 1)
    with eng.Fori(2, tiles - AHEAD) as j:
        body(j, AHEAD + 1)
    for left in range(AHEAD, 0, -1):
        body(tiles - left, left)


def has_tile(j, ahead, left):
    return ahead < left and (not isinstance(j, int) or j + ahead >= 0)


def flamingo_block(nc, x, x_t, ctx_t, g_xattn, g_ffn, wq_t, wk_t, wv, gate_w, gate_b,
                   w1, w2, w3, b1, b2, b3, out, xn2_dram, slot_tok, slot_w):
    x_v = x.rearrange("b (c p) d -> b p c d", p=P)
    out_v = out.rearrange("b (c p) d -> b p c d", p=P)
    xn2_v = xn2_dram.rearrange("(b c p) d -> b p c d", c=RC, p=P)
    w_dram = [w1, w2, w3]
    b_dram = [b1, b2, b3]

    with ExitStack() as ctx:
        def sem(name):
            return ctx.enter_context(nc.semaphore(name))

        def alloc(stack, name, shape, dt):
            return stack.enter_context(nc.sbuf_tensor(name, shape, dt))

        ident = alloc(ctx, "ident", [P, P], F32)
        tri = alloc(ctx, "tri", [P, P], F32)
        ones = alloc(ctx, "ones", [P, P], F32)
        tg_attn = alloc(ctx, "tg_attn", [P, 1], F32)
        tg_ffn = alloc(ctx, "tg_ffn", [P, 1], F32)
        g_raw = alloc(ctx, "g_raw", [P, 2], F32)
        wq_mean = alloc(ctx, "wq_mean", [P, DC, 2], F32)
        iota_i = alloc(ctx, "iota_i", [P, E], I32)
        ebase_i = alloc(ctx, "ebase_i", [P, E], I32)
        jidx_i = alloc(ctx, "jidx_i", [P, NT], I32)
        iota_e = alloc(ctx, "iota_e", [P, E], F32)
        ebase = alloc(ctx, "ebase", [P, E], F32)
        jidx = alloc(ctx, "jidx", [P, NT], F32)
        tokall = alloc(ctx, "tokall", [P, B * RC], U32)
        base = alloc(ctx, "base", [P, RC, E], F32)
        table = alloc(ctx, "table", [P, NT, 2], I32)
        extra = alloc(ctx, "extra", [P, 1], I32)
        tile_onehot = alloc(ctx, "tile_onehot", [P, E, NT], F32)
        vparts = alloc(ctx, "vparts", [P, NT, DC], F32)
        ind16 = alloc(ctx, "ind16", [2 * E, TOK], F32R)

        with ExitStack() as tmp:
            alloc(tmp, "x_head_room", [P, 2 * RC * D], F32)
            wq_raw = alloc(tmp, "wq_raw", [P, DC, D], F32)
            wk_raw = alloc(tmp, "wk_raw", [P, DC, D], F32)
            wv_raw = alloc(tmp, "wv_raw", [P, DC, D], F32)
            wq_hi = alloc(tmp, "wq_hi", [P, DC, D], F32R)
            wq_lo = alloc(tmp, "wq_lo", [P, DC, D], F32R)
            wk_hi = alloc(tmp, "wk_hi", [P, DC, D], F32R)
            wk_lo = alloc(tmp, "wk_lo", [P, DC, D], F32R)
        x_all = alloc(ctx, "x_all", [P, B, RC, D], F32)

        with ExitStack() as ph:
            a_hi = alloc(ph, "a_hi", [P, DC, D], F32R)
            a_lo = alloc(ph, "a_lo", [P, DC, D], F32R)
            wv_hi = alloc(ph, "wv_hi", [P, DC, D], F32R)
            wv_lo = alloc(ph, "wv_lo", [P, DC, D], F32R)
            c_raw = alloc(ph, "c_raw", [P, DC, S], F32)
            c_hi = alloc(ph, "c_hi", [P, DC, S], F32R)
            c_lo = alloc(ph, "c_lo", [P, DC, S], F32R)
            xt_raw = alloc(ph, "xt_raw", [P, DC, S], F32)
            xt_hi = alloc(ph, "xt_hi", [P, DC, S], F32R)
            xt_lo = alloc(ph, "xt_lo", [P, DC, S], F32R)
            qa_hi = alloc(ph, "qa_hi", [P, DC, S], F32R)
            qa_lo = alloc(ph, "qa_lo", [P, DC, S], F32R)
            v_hi = alloc(ph, "v_hi", [P, RC, D], F32R)
            v_lo = alloc(ph, "v_lo", [P, RC, D], F32R)
            pexp = alloc(ph, "pexp", [P, RC, S], F32)
            pt_hi = alloc(ph, "pt_hi", [P, RC, S], F32R)
            pt_lo = alloc(ph, "pt_lo", [P, RC, S], F32R)
            xn2 = alloc(ph, "xn2", [P, RC, D], F32)
            gt_hi = alloc(ph, "gt_hi", [P, DC, S], F32R)
            gt_lo = alloc(ph, "gt_lo", [P, DC, S], F32R)
            gw_raw = alloc(ph, "gw_raw", [P, DC, E], F32)
            gw_hi = alloc(ph, "gw_hi", [P, DC, E], F32R)
            gw_lo = alloc(ph, "gw_lo", [P, DC, E], F32R)
            gb = alloc(ph, "gb", [E, 1], F32)
            st1 = alloc(ph, "st1", [P, RC, 6], F32)
            mv1 = alloc(ph, "mv1", [P, RC, 2], F32)
            rn1 = alloc(ph, "rn1", [P, 4, RC], F32)
            st2 = alloc(ph, "st2", [P, RC, 6], F32)
            mv2 = alloc(ph, "mv2", [P, RC, 2], F32)
            rn2 = alloc(ph, "rn2", [P, 4, RC], F32)
            mhalf = alloc(ph, "mhalf", [P, RC], F32)
            smax = alloc(ph, "smax", [P, RC], F32)
            nbias = alloc(ph, "nbias", [P, RC], F32)
            ssum = alloc(ph, "ssum", [P, RC], F32)
            rsum = alloc(ph, "rsum", [P, RC], F32)
            coef = alloc(ph, "coef", [P, RC], F32)
            logit = alloc(ph, "logit", [E, S], F32)
            gmax = alloc(ph, "gmax", [E, 2], F32)
            gexp = alloc(ph, "gexp", [E, S], F32)
            gsum = alloc(ph, "gsum", [E, 2], F32)
            probs = alloc(ph, "probs", [E, S], F32)
            pr = alloc(ph, "pr", [P, RC, E], F32)
            top = alloc(ph, "top", [P, RC, E], F32)
            topi = alloc(ph, "topi", [P, RC, E], U32)
            topf = alloc(ph, "topf", [P, RC, TOPK], F32)
            oh = alloc(ph, "oh", [P, RC, TOPK, E], F32)
            ind2 = alloc(ph, "ind2", [P, RC, 2, E], F32)
            full = alloc(ph, "full", [P, RC, E], F32)
            prod = alloc(ph, "prod", [P, RC, TOPK, E], F32)
            pos = alloc(ph, "pos", [P, RC, TOPK], F32)
            slot_u = alloc(ph, "slot_u", [P, RC * TOPK], U32)
            tok_u = alloc(ph, "tok_u", [P, RC], U32)
            w_out = alloc(ph, "w_out", [P, RC * TOPK], F32)
            zeros = alloc(ph, "zeros", [P, NSLOT // P], F32)
            cnt = alloc(ph, "cnt", [P, E], F32)
            cnt_i = alloc(ph, "cnt_i", [P, 2, E], I32)
            ntile = alloc(ph, "ntile", [P, E], F32)
            cum = alloc(ph, "cum", [P, E], F32)
            onesE = alloc(ph, "onesE", [P, E], F32)
            le = alloc(ph, "le", [P, NT, E - 1], F32)
            lep = alloc(ph, "lep", [P, NT, E - 1], F32)
            tile_e = alloc(ph, "tile_e", [P, NT], F32)
            tile_prev = alloc(ph, "tile_prev", [P, NT], F32)
            row1 = alloc(ph, "row1", [P, NT], F32)
            row2 = alloc(ph, "row2", [P, NT], F32)
            row3 = alloc(ph, "row3", [P, NT], F32)

        with ExitStack() as ph:
            w_raw = [alloc(ph, f"w_raw{n}", [P, DC, D], F32) for n in range(3)]
            w_hi = [alloc(ph, f"w_hi{n}", [P, DC, D], F32R) for n in range(3)]
            w_lo = [alloc(ph, f"w_lo{n}", [P, DC, D], F32R) for n in range(3)]
            bias = [alloc(ph, f"bias{n}", [P, DC], F32) for n in range(3)]
            idx = alloc(ph, "idx", [P, TH], U32)
            xg = alloc(ph, "xg", [P, TH, D], F32)
            et_hi = alloc(ph, "et_hi", [P, DC, TILE], F32R)
            et_lo = alloc(ph, "et_lo", [P, DC, TILE], F32R)
            h = [alloc(ph, f"h{n}", [P, DC, TILE], F32) for n in range(2)]
            h_hi = [alloc(ph, f"h_hi{n}", [P, DC, TILE], F32R) for n in range(2)]
            h_lo = [alloc(ph, f"h_lo{n}", [P, DC, TILE], F32R) for n in range(2)]
            wb = alloc(ph, "wb", [P, TILE], F32)
            junk = alloc(ph, "junk", [P, TILE], F32)
            nb3 = alloc(ph, "nb3", [P, DC], F32)
            wsum = alloc(ph, "wsum", [P, 1], F32)
            acc = alloc(ph, "acc", [P, DC], F32)
            vprod = alloc(ph, "vprod", [P, E, DC, NT], F32)
            vt = alloc(ph, "vt", [P, E, DC], F32)
            vs = alloc(ph, "vs", [P, E, DC], F32)
            vs_hi = alloc(ph, "vs_hi", [P, E, DC], F32R)
            vhl = alloc(ph, "vhl", [P, DC, 2, E], F32)
            v_rows = alloc(ph, "v_rows", [P, 2, D], F32)
            v16 = alloc(ph, "v16", [2 * E, D], F32R)

        bank = [ctx.enter_context(nc.psum_tensor(f"bank{n}", [P, 512], F32)) for n in range(8)]
        bS = bank[0]
        bQ = [bank[1], bank[2]]
        bV = [bank[3], bank[4]]
        bG = [bank[5], bank[6]]
        bR = bank[7]
        bA = [bank[3], bank[4], bank[5], bank[6]]
        bL = [[bank[0], bank[1]], [bank[2], bank[3]], [bank[4], bank[5]]]
        bT = [bank[6], bank[7]]
        R_LOGIT = bR[0:E, 0:S]
        R_IND = bR[0:2 * E, 0:S]
        R_PROB = bR[:, 256:256 + RC * E]
        R_RANK = bR[:, 288:288 + RC * E]
        R_TOT = bR[:, 304:304 + RC * E]

        s_iota = sem("s_iota")
        s_pool_const = sem("s_pool_const")
        s_conv = sem("s_conv")
        s_zero = sem("s_zero")
        s_zero_dma = sem("s_zero_dma")
        s_small = sem("s_small")
        s_tanh = sem("s_tanh")
        s_wq_in = [sem(f"s_wq_in{n}") for n in range(DC)]
        s_wk_in = [sem(f"s_wk_in{n}") for n in range(DC)]
        s_wv_in = sem("s_wv_in")
        s_wq_hi, s_wk_hi, s_wv_hi, s_gw_hi = sem("s_wq_hi"), sem("s_wk_hi"), sem("s_wv_hi"), sem("s_gw_hi")
        s_wq_lo, s_wk_lo, s_wv_lo, s_gw_lo = sem("s_wq_lo"), sem("s_wk_lo"), sem("s_wv_lo"), sem("s_gw_lo")
        a_mm, a_his, a_los = sem("a_mm"), sem("a_his"), sem("a_los")
        x_in, c_in = sem("x_in"), sem("c_in")
        ln1_stat, ln1_small, xt_in = sem("ln1_stat"), sem("ln1_small"), sem("xt_in")
        s_wq_sum, s_wq_mean, s_wq_c = sem("s_wq_sum"), sem("s_wq_mean"), sem("s_wq_c")
        ln2_stat, ln2_small, xn2_ready = sem("ln2_stat"), sem("ln2_small"), sem("xn2_ready")
        c_his, c_los = sem("c_his"), sem("c_los")
        xt_his, xt_los = sem("xt_his"), sem("xt_los")
        qa_done, qa_his, qa_los = sem("qa_done"), sem("qa_his"), sem("qa_los")
        sc_done, nbias_ready, exp_done = sem("sc_done"), sem("nbias_ready"), sem("exp_done")
        tp_done, pt_his, pt_los = sem("tp_done"), sem("pt_his"), sem("pt_los")
        v_done, v_his, v_los = sem("v_done"), sem("v_his"), sem("v_los")
        pv_done, coef_ready, x2_done, xn2_out = sem("pv_done"), sem("coef_ready"), sem("x2_done"), sem("xn2_out")
        tg_done, gt_his, gt_los = sem("tg_done"), sem("gt_his"), sem("gt_los")
        gate_done, gmax_ready, gexp_done, probs_ready = sem("gate_done"), sem("gmax_ready"), sem("gexp_done"), sem("probs_ready")
        pt8_done, top_step, rank_done, slot_step = sem("pt8_done"), sem("top_step"), sem("rank_done"), sem("slot_step")
        tok_sent, w_sent = sem("tok_sent"), sem("w_sent")
        table_step = sem("table_step")
        w_in = [sem(f"w_in{n}") for n in range(3)]
        b_in = [sem(f"b_in{n}") for n in range(3)]
        w_his = [sem(f"w_his{n}") for n in range(3)]
        w_los = [sem(f"w_los{n}") for n in range(3)]
        idx_in, wb_in, gathered = sem("idx_in"), sem("wb_in"), sem("gathered")
        te_done, et_his, et_los = sem("te_done"), sem("et_his"), sem("et_los")
        l_done = [sem(f"l_done{n}") for n in range(3)]
        relu_done = [sem(f"relu_done{n}") for n in range(2)]
        h_his = [sem(f"h_his{n}") for n in range(2)]
        h_los = [sem(f"h_los{n}") for n in range(2)]
        bn_step, gate_step = sem("bn_step"), sem("gate_step")
        tail_small, wsum_step, part_done = sem("tail_small"), sem("wsum_step"), sem("part_done")
        v_step, vt_done, v16_ready = sem("v_step"), sem("vt_done"), sem("v16_ready")
        o_done, out_sent = sem("o_done"), sem("out_sent")
        res_dve, res_copied, res_pool = sem("res_dve"), sem("res_copied"), sem("res_pool")

        NTOP, NSTEP, NTAB = 9, 9, 15

        waited = {name: sem(f"waited_{name}") for name in ("sp", "act", "pool", "dve", "pe")}

        def wait_alone(eng, name):
            eng.sem_inc(waited[name], 1)

        def tiles_in_use(eng):
            eng.wait_ge(table_step, NTAB)
            return eng.value_load(extra[0:1, 0:1], min_val=0, max_val=NT - NT_MIN) + NT_MIN

        block = ctx.enter_context(nc.Block())

        @block.sync
        def _(sp):
            for n in range(DC):
                sp.dma_start(wq_raw[:, n], wq_t[:, n]).then_inc(s_wq_in[n], 16)
                sp.dma_start(wk_raw[:, n], wk_t[:, n]).then_inc(s_wk_in[n], 16)
            sp.dma_start(x_all[:, 0], x_v[0]).then_inc(x_in, 16)
            sp.dma_start(g_raw[:, 0:1], g_xattn.rearrange("(a n) -> a n", a=1).broadcast_to([P, 1])).then_inc(s_small, 16)
            sp.dma_start(g_raw[:, 1:2], g_ffn.rearrange("(a n) -> a n", a=1).broadcast_to([P, 1])).then_inc(s_small, 16)
            sp.dma_start(gw_raw[:], gate_w).then_inc(s_small, 16)
            sp.dma_start(gb[:], gate_b.rearrange("(e n) -> e n", n=1)).then_inc(s_small, 16)
            sp.dma_start(wv_raw[:], wv).then_inc(s_wv_in, 16)
            sp.wait_ge(s_zero, 1)
            sp.dma_start(slot_tok.rearrange("(p n) a -> p (n a)", p=P), zeros[:].bitcast(U32)).then_inc(s_zero_dma, 16)
            sp.dma_start(slot_w.rearrange("(p n) a -> p (n a)", p=P), zeros[:]).then_inc(s_zero_dma, 16)

            sp.dma_start(xt_raw[:], x_t[0]).then_inc(xt_in, 16)

            def batch(b):
                if exists(b + 1, B):
                    need(sp, c_los, b + 1)
                    sp.dma_start(c_raw[:], ctx_t[b + 1] if isinstance(b, int) else
                                 ctx_t[bass.ds(b + 1, 1)].rearrange("a p c s -> (a p) c s")).then_inc(c_in, 16)
                if exists(b + 3, B):
                    need(sp, x_in, (b + 3) * 16)
                    if isinstance(b, int) and b + 3 == 2:
                        sp.wait_ge(a_mm, DC)
                        sp.wait_ge(s_wv_lo, 1)
                    sp.dma_start(x_all[:, bass.ds(b + 3, 1)], x_v[bass.ds(b + 3, 1)].rearrange("a p c d -> p a c d")
                                 ).then_inc(x_in, 16)
                if exists(b - 1, B):
                    need(sp, xn2_ready, RC * b)
                    sp.dma_start(xn2_v[bass.ds(b - 1, 1)].rearrange("a p c d -> p a c d"),
                                 xn2[:].rearrange("p (a c) d -> p a c d", a=1)).then_inc(xn2_out, 16)
                if exists(b + 2, B) and not (isinstance(b, int) and b + 2 == 0):
                    need(sp, xt_los, b + 2)
                    sp.dma_start(xt_raw[:], x_t[b + 2] if isinstance(b, int) else
                                 x_t[bass.ds(b + 2, 1)].rearrange("a p c s -> (a p) c s")).then_inc(xt_in, 16)

            batch(-2)
            pipeline(sp, batch, *BATCHES)

            tiles = tiles_in_use(sp)

            def load_w(n, m):
                need(sp, w_los[n], m)
                wait_alone(sp, "sp")
                e = sp.value_load(table[0:1, bass.ds(m, 1), 0:1], min_val=0, max_val=E - 1)
                sp.dma_start(w_raw[n][:], w_dram[n][bass.ds(e, 1)].rearrange("a p c d -> (a p) c d")
                             ).then_inc(w_in[n], 16)

            def load_b(n, m):
                wait_alone(sp, "sp")
                e = sp.value_load(table[0:1, bass.ds(m, 1), 0:1], min_val=0, max_val=E - 1)
                sp.dma_start(bias[n][:], b_dram[n][bass.ds(e, 1)].rearrange("a p c -> (a p) c")
                             ).then_inc(b_in[n], 16)

            def load_idx(m):
                need(sp, gathered, 16 * TH * m)
                wait_alone(sp, "sp")
                r = sp.value_load(table[0:1, bass.ds(m, 1), 1:2], min_val=0, max_val=NSLOT - TILE)
                sp.dma_start(idx[:], slot_tok[bass.ds(r, TILE)].rearrange("(p h) a -> p (h a)", p=P)
                             ).then_inc(idx_in, 16)

            def tile(j, left):
                if has_tile(j, 1, left):
                    if not isinstance(j, int) or j + 1 > 0:
                        load_w(2, j + 1)
                    need(sp, relu_done[1], DC * (j + 1))
                    load_b(1, j + 1)
                if has_tile(j, 2, left):
                    if not isinstance(j, int) or j + 2 > 0:
                        load_w(1, j + 2)
                    need(sp, relu_done[0], DC * (j + 2))
                    load_b(0, j + 2)
                if has_tile(j, 3, left):
                    if not isinstance(j, int) or j + 3 > 0:
                        load_w(0, j + 3)
                if has_tile(j, 1, left):
                    need(sp, part_done, j + 1)
                    load_b(2, j + 1)
                    wait_alone(sp, "sp")
                    r = sp.value_load(table[0:1, bass.ds(j + 1, 1), 1:2], min_val=0, max_val=NSLOT - TILE)
                    sp.dma_start(wb[:], slot_w[bass.ds(r, TILE)].rearrange("n a -> a n").broadcast_to([P, TILE])
                                 ).then_inc(wb_in, 16)
                if has_tile(j, 4, left) and (not isinstance(j, int) or j + 4 > 0):
                    load_idx(j + 4)

            load_w(0, 0)
            sp.wait_ge(tok_sent, 16 * RC * TOPK * B)
            load_idx(0)
            load_w(1, 0)
            load_w(2, 0)
            sp.wait_ge(w_sent, 16 * RC * TOPK * B)
            tile_pipeline(sp, tile, tiles)

            for b in range(B):
                sp.wait_ge(res_dve, RC * (b + 1) - (b + 1) // 2)
                if b % 2 == 1:
                    sp.wait_ge(res_pool, (b + 1) // 2)
                sp.dma_start(out_v[b], x_all[:, b]).then_inc(out_sent, 16)
            sp.wait_ge(out_sent, 16 * B)

        @block.gpsimd
        def _(pool):
            pool.memset(zeros[:], 0.0).then_inc(s_zero, 1)
            pool.memset(ident[:], 0.0).then_inc(s_iota, 1)
            pool.memset(ones[:], 1.0).then_inc(s_pool_const, 1)
            pool.memset(tri[:], 1.0).then_inc(s_iota, 1)
            pool.memset(mhalf[:], -0.5).then_inc(s_pool_const, 1)
            pool.memset(onesE[:], 1.0).then_inc(s_pool_const, 1)
            pool.wait_ge(s_iota, 2)
            pool.affine_select(out=ident[:], in_=ident[:], compare_op=ALU.not_equal, fill=1.0, base=0,
                               pattern=[[-1, P]], channel_multiplier=1).then_inc(s_pool_const, 1)
            pool.affine_select(out=tri[:], in_=tri[:], compare_op=ALU.is_gt, fill=0.0, base=0,
                               pattern=[[1, P]], channel_multiplier=-1).then_inc(s_pool_const, 1)
            pool.iota(iota_i[:], pattern=[[1, E]], base=0, channel_multiplier=0).then_inc(s_iota, 1)
            pool.iota(ebase_i[:], pattern=[[REGION, E]], base=0, channel_multiplier=0).then_inc(s_iota, 1)
            pool.iota(jidx_i[:], pattern=[[1, NT]], base=0, channel_multiplier=0).then_inc(s_iota, 1)
            pool.iota(tokall[:], pattern=[[P, B * RC]], base=0, channel_multiplier=1).then_inc(s_iota, 1)
            pool.wait_ge(s_pool_const, 5)

            def inverse_deviation(mv, rn, done, m):
                wait_alone(pool, "pool")
                pool.tensor_scalar(rn[:, 0, :], mv[:, :, 1], EPS, None, ALU.add).then_inc(done, 1)
                pool.wait_ge(done, 4 * m + 1)
                pool.tensor_tensor(rn[:, 1, :], rn[:, 0, :], mhalf[:], ALU.pow).then_inc(done, 1)
                pool.wait_ge(done, 4 * m + 2)
                wait_alone(pool, "pool")

            def batch(b):
                if exists(b + 1, B):
                    need(pool, ln1_stat, RC * (b + 2))
                    need(pool, exp_done, RC * (b + 1))
                    inverse_deviation(mv1, rn1, ln1_small, b + 1)
                    pool.tensor_scalar(rn1[:, 2, :], rn1[:, 1, :], SCALE, None, ALU.mult).then_inc(ln1_small, 1)
                    pool.tensor_scalar(rn1[:, 3, :], rn1[:, 1, :], -SCALE, None, ALU.mult).then_inc(ln1_small, 1)
                if exists(b + 1, B):
                    need(pool, c_his, b + 2)
                    pool.tensor_tensor(c_lo[:], c_raw[:], c_hi[:].bitcast(F32), ALU.subtract).then_inc(c_los, 1)
                if exists(b - 2, B):
                    need(pool, slot_step, NSTEP * (b - 1))
                    if isinstance(b, int) and b == 2:
                        pool.wait_ge(s_zero_dma, 32)
                    wait_alone(pool, "pool")
                    for n in range(RC * TOPK):
                        pool.indirect_dma_start(slot_tok, bass.IndirectOffsetOnAxis(ap=slot_u[:, n:n + 1], axis=0),
                                                tok_u[:, n // TOPK:n // TOPK + 1], None).then_inc(tok_sent, 16)
                    for n in range(RC * TOPK):
                        pool.indirect_dma_start(slot_w, bass.IndirectOffsetOnAxis(ap=slot_u[:, n:n + 1], axis=0),
                                                w_out[:, n:n + 1], None).then_inc(w_sent, 16)
                if exists(b, B):
                    need(pool, ln2_stat, RC * (b + 1))
                    need(pool, xn2_ready, RC * b)
                    inverse_deviation(mv2, rn2, ln2_small, b)
                    pool.tensor_scalar(rn2[:, 2, :], mv2[:, :, 0], -1.0, None, ALU.mult).then_inc(ln2_small, 1)
                    pool.wait_ge(ln2_small, 4 * b + 3)
                    pool.tensor_tensor(rn2[:, 3, :], rn2[:, 2, :], rn2[:, 1, :], ALU.mult).then_inc(ln2_small, 1)

            pipeline(pool, batch, *BATCHES)

            pool.wait_ge(xn2_out, 16 * B)

            def tile(j, left):
                if has_tile(j, 0, left):
                    for k in range(2):
                        pool.wait_ge(h_his[1], 2 * j + k + 1)
                        pool.tensor_tensor(h_lo[1][:, 2 * k:2 * k + 2], h[1][:, 2 * k:2 * k + 2],
                                           h_hi[1][:, 2 * k:2 * k + 2].bitcast(F32), ALU.subtract).then_inc(h_los[1], 1)
                if has_tile(j, 1, left):
                    for k in range(2):
                        pool.wait_ge(h_his[0], 2 * (j + 1) + k + 1)
                        pool.tensor_tensor(h_lo[0][:, 2 * k:2 * k + 2], h[0][:, 2 * k:2 * k + 2],
                                           h_hi[0][:, 2 * k:2 * k + 2].bitcast(F32), ALU.subtract).then_inc(h_los[0], 1)
                if has_tile(j, 3, left):
                    need(pool, idx_in, 16 * (j + 4))
                    need(pool, te_done, 2 * (j + 3))
                    wait_alone(pool, "pool")
                    for t in range(TH):
                        pool.indirect_dma_start(xg[:, t], None, xn2_dram,
                                                bass.IndirectOffsetOnAxis(ap=idx[:, t:t + 1], axis=0)
                                                ).then_inc(gathered, 16)

            tile_pipeline(pool, tile, tiles_in_use(pool))

            for n in range(3, B * RC, 4):
                pool.wait_ge(res_copied, n // 4 + 1)
                row = x_all[:, n // RC, n % RC]
                pool.tensor_tensor(row, v_rows[:, (n // 4) % 2], row, ALU.add).then_inc(res_pool, 1)

        @block.scalar
        def _(act):
            def batch(b):
                if exists(b, B):
                    need(act, nbias_ready, 2 * (b + 1))
                    need(act, tp_done, b)
                    for c in range(RC):
                        act.activation(pexp[:, c], bS[:, c * S:(c + 1) * S], ACT.Exp, bias=nbias[:, c:c + 1],
                                       scale=rn1[:, 2, c:c + 1], accum_out=ssum[:, c:c + 1]).then_inc(exp_done, 1)
                if exists(b + 1, B):
                    act.wait_ge(xt_in, 16 * (b + 2))
                    need(act, qa_done, 2 * (b + 1))
                    act.activation(xt_hi[:], xt_raw[:], ACT.Copy).then_inc(xt_his, 1)
                if exists(b, B):
                    need(act, pv_done, 2 * b)
                    for k in range(RC):
                        need(act, v_done, 2 * b + k + 1)
                        act.activation(v_hi[:, k], bV[k][:], ACT.Copy).then_inc(v_his, 1)
                if exists(b + 1, B):
                    need(act, c_in, 16 * (b + 2))
                    need(act, v_done, 2 * (b + 1))
                    act.activation(c_hi[:], c_raw[:], ACT.Copy).then_inc(c_his, 1)
                if exists(b, B):
                    need(act, tp_done, b + 1)
                    act.activation(pt_hi[:], bS[:].rearrange("p (c s) -> p c s", c=RC), ACT.Copy).then_inc(pt_his, 1)
                if exists(b - 1, B):
                    need(act, gate_done, b - 1)
                    for k in range(2):
                        need(act, tg_done, 2 * (b - 1) + k + 1)
                        act.activation(gt_hi[:, 2 * k:2 * k + 2], bG[k][:].rearrange("p (c s) -> p c s", c=2),
                                       ACT.Copy).then_inc(gt_his, 1)
                if exists(b + 1, B):
                    need(act, sc_done, b + 1)
                    for k in range(2):
                        need(act, qa_done, 2 * (b + 1) + k + 1)
                        act.activation(qa_hi[:, 2 * k:2 * k + 2], bQ[k][:].rearrange("p (c s) -> p c s", c=2),
                                       ACT.Copy).then_inc(qa_his, 1)
                if exists(b - 1, B):
                    need(act, gmax_ready, 2 * b)
                    act.activation(gexp[:], logit[:], ACT.Exp, bias=gmax[:, 1:2], accum_out=gsum[:, 0:1]
                                   ).then_inc(gexp_done, 1)
                if exists(b, B):
                    need(act, ln2_small, 4 * (b + 1))
                    need(act, tg_done, 2 * b)
                    need(act, xn2_out, 16 * b)
                    for c in range(RC):
                        act.activation(xn2[:, c], x_all[:, bass.ds(b, 1), c].rearrange("p a d -> p (a d)"),
                                       ACT.Identity, bias=rn2[:, 3, c:c + 1], scale=rn2[:, 1, c:c + 1]
                                       ).then_inc(xn2_ready, 1)

            for n in range(DC):
                act.wait_ge(s_wq_mean, n + 1)
                act.activation(wq_raw[:, n], wq_raw[:, n], ACT.Identity, bias=wq_mean[:, n, 1:2]).then_inc(s_wq_c, 1)
                act.wait_ge(s_wq_c, n + 1)
                act.activation(wq_hi[:, n], wq_raw[:, n], ACT.Copy).then_inc(s_wq_hi, 1)
            act.wait_ge(s_wv_in, 16)
            act.activation(wv_hi[:], wv_raw[:], ACT.Copy).then_inc(s_wv_hi, 1)
            for n in range(DC):
                act.wait_ge(a_mm, n + 1)
                act.activation(a_hi[:, n], bA[n][:], ACT.Copy).then_inc(a_his, 1)
            act.wait_ge(s_small, 64)
            act.activation(tg_attn[:], g_raw[:, 0:1], ACT.Tanh).then_inc(s_tanh, 1)
            act.activation(tg_ffn[:], g_raw[:, 1:2], ACT.Tanh).then_inc(s_tanh, 1)
            act.activation(gw_hi[:], gw_raw[:], ACT.Copy).then_inc(s_gw_hi, 1)
            pipeline(act, batch, *BATCHES)

            def split_w(n, m):
                act.wait_ge(w_in[n], 16 * (m + 1))
                need(act, l_done[n], 2 * m)
                act.activation(w_hi[n][:], w_raw[n][:], ACT.Copy).then_inc(w_his[n], 1)

            def relu(n, m):
                act.wait_ge(b_in[n], 16 * (m + 1))
                for oc in range(DC):
                    if oc % 2 == 0:
                        act.wait_ge(l_done[n], 2 * m + oc // 2 + 1)
                        need(act, h_los[n], 2 * (m - 1) + oc // 2 + 1)
                    act.activation(h[n][:, oc], bL[n][oc // 2][:, (oc % 2) * TILE:(oc % 2 + 1) * TILE], ACT.Relu,
                                   bias=bias[n][:, oc:oc + 1]).then_inc(relu_done[n], 1)

            def tile(j, left):
                if has_tile(j, 0, left):
                    split_w(2, j)
                    relu(1, j)
                if has_tile(j, 1, left):
                    split_w(1, j + 1)
                    relu(0, j + 1)
                if has_tile(j, 2, left):
                    split_w(0, j + 2)
                    need(act, l_done[0], 2 * (j + 2))
                    for k in range(2):
                        act.wait_ge(te_done, 2 * (j + 2) + k + 1)
                        act.activation(et_hi[:, 2 * k:2 * k + 2], bT[k][:].rearrange("p (c s) -> p c s", c=2),
                                       ACT.Copy).then_inc(et_his, 1)

            tile_pipeline(act, tile, tiles_in_use(act))

            for n in range(3, B * RC, 4):
                act.wait_ge(o_done, n + 1)
                need(act, res_pool, n // 4 - 1)
                act.activation(v_rows[:, (n // 4) % 2], bank[n % 8][:], ACT.Copy).then_inc(res_copied, 1)

        @block.vector
        def _(dve):
            dve.wait_ge(s_iota, 6)
            dve.tensor_copy(iota_e[:], iota_i[:]).then_inc(s_conv, 1)
            dve.tensor_copy(ebase[:], ebase_i[:]).then_inc(s_conv, 1)
            dve.tensor_copy(jidx[:], jidx_i[:]).then_inc(s_conv, 1)
            dve.tensor_copy(base[:, 0], ebase_i[:]).then_inc(s_conv, 1)
            dve.wait_ge(s_conv, 4)

            def stats(src_batch, st, mv, done, step_sem_base):
                wait_alone(dve, "dve")
                for c in range(RC):
                    dve.bn_stats(st[:, c], x_all[:, bass.ds(src_batch, 1), c].rearrange("p a d -> p (a d)")
                                 ).then_inc(bn_step, 1)
                dve.wait_ge(bn_step, step_sem_base + RC)
                wait_alone(dve, "dve")
                for c in range(RC):
                    dve.bn_aggr(mv[:, c], st[:, c]).then_inc(done, 1)

            def low(dst, src, hi, done):
                dve.tensor_tensor(dst, src, hi.bitcast(F32), ALU.subtract).then_inc(done, 1)

            def two(bk):
                return bk[:].rearrange("p (c s) -> p c s", c=2)

            def batch(b):
                if exists(b, B):
                    need(dve, sc_done, b + 1)
                    dve.tensor_reduce(smax[:], bS[:].rearrange("p (c s) -> p c s", c=RC), AX_X, ALU.max
                                      ).then_inc(nbias_ready, 1)
                    dve.wait_ge(nbias_ready, 2 * b + 1)
                    need(dve, ln1_small, 4 * (b + 1))
                    dve.tensor_tensor(nbias[:], smax[:], rn1[:, 3, :], ALU.mult).then_inc(nbias_ready, 1)
                if exists(b + 1, B):
                    need(dve, x_in, 16 * (b + 2))
                    need(dve, ln1_small, 4 * (b + 1))
                    stats(b + 1, st1, mv1, ln1_stat, bn_before(b + 1, True))
                    need(dve, xt_his, b + 2)
                    low(xt_lo[:], xt_raw[:], xt_hi[:], xt_los)
                if exists(b, B):
                    for k in range(RC):
                        need(dve, v_his, 2 * b + k + 1)
                        low(v_lo[:, k], bV[k][:], v_hi[:, k], v_los)
                    need(dve, pt_his, b + 1)
                    low(pt_lo[:], two(bS), pt_hi[:], pt_los)
                if exists(b - 1, B):
                    for k in range(2):
                        need(dve, gt_his, 2 * (b - 1) + k + 1)
                        low(gt_lo[:, 2 * k:2 * k + 2], two(bG[k]), gt_hi[:, 2 * k:2 * k + 2], gt_los)
                if exists(b - 2, B):
                    m = b - 2
                    need(dve, rank_done, m + 1)
                    dve.tensor_copy(ind16[:, bass.ds(m * S, S)], R_IND).then_inc(slot_step, 1)
                    dve.tensor_tensor(base[:, 1], base[:, 0], R_TOT[:, 0:E], ALU.add).then_inc(slot_step, 1)
                    dve.wait_ge(slot_step, NSTEP * m + 2)
                    dve.tensor_tensor(full[:].rearrange("p c e -> p (c e)"), R_RANK,
                                      base[:].rearrange("p c e -> p (c e)"), ALU.add).then_inc(slot_step, 1)
                    dve.wait_ge(slot_step, NSTEP * m + 3)
                    dve.tensor_tensor(base[:, 0], base[:, 1], R_TOT[:, E:2 * E], ALU.add).then_inc(slot_step, 1)
                    dve.tensor_tensor(prod[:], oh[:], full[:].unsqueeze(2).broadcast_to([P, RC, TOPK, E]), ALU.mult
                                      ).then_inc(slot_step, 1)
                    dve.wait_ge(slot_step, NSTEP * m + 5)
                    dve.tensor_reduce(pos[:], prod[:], AX_X, ALU.add).then_inc(slot_step, 1)
                    dve.wait_ge(slot_step, NSTEP * m + 6)
                    need(dve, tok_sent, 16 * RC * TOPK * m)
                    need(dve, w_sent, 16 * RC * TOPK * m)
                    dve.tensor_copy(slot_u[:], pos[:].rearrange("p c k -> p (c k)")).then_inc(slot_step, 1)
                    dve.tensor_copy(tok_u[:], tokall[:, bass.ds(m * RC, RC)]).then_inc(slot_step, 1)
                    dve.tensor_copy(w_out[:].rearrange("p (c k) -> p c k", c=RC), top[:, :, 0:TOPK]
                                    ).then_inc(slot_step, 1)
                if exists(b + 1, B):
                    for k in range(2):
                        need(dve, qa_his, 2 * (b + 1) + k + 1)
                        low(qa_lo[:, 2 * k:2 * k + 2], two(bQ[k]), qa_hi[:, 2 * k:2 * k + 2], qa_los)
                if exists(b - 1, B):
                    m = b - 1
                    need(dve, gate_done, m + 1)
                    dve.tensor_scalar(logit[:], R_LOGIT, gb[:, 0:1], None, ALU.add).then_inc(gate_step, 1)
                    dve.wait_ge(gate_step, 2 * m + 1)
                    dve.tensor_reduce(gmax[:, 0:1], logit[:], AX_X, ALU.max).then_inc(gmax_ready, 1)
                    dve.wait_ge(gmax_ready, 2 * m + 1)
                    dve.tensor_scalar(gmax[:, 1:2], gmax[:, 0:1], -1.0, None, ALU.mult).then_inc(gmax_ready, 1)
                    dve.wait_ge(gexp_done, m + 1)
                    dve.reciprocal(gsum[:, 1:2], gsum[:, 0:1]).then_inc(gate_step, 1)
                    dve.wait_ge(gate_step, 2 * m + 2)
                    dve.tensor_scalar(probs[:], gexp[:], gsum[:, 1:2], None, ALU.mult).then_inc(probs_ready, 1)
                if exists(b, B):
                    need(dve, exp_done, RC * (b + 1))
                    dve.reciprocal(rsum[:], ssum[:]).then_inc(coef_ready, 1)
                    dve.wait_ge(coef_ready, 2 * b + 1)
                    dve.tensor_scalar(coef[:], rsum[:], tg_attn[:, 0:1], None, ALU.mult).then_inc(coef_ready, 1)
                    dve.wait_ge(coef_ready, 2 * b + 2)
                    for c in range(RC):
                        row = x_all[:, bass.ds(b, 1), c].rearrange("p a d -> p (a d)")
                        need(dve, pv_done, 2 * b + c + 1)
                        dve.scalar_tensor_tensor(out=row, in0=bV[c][:], scalar=coef[:, c:c + 1], in1=row,
                                                 op0=ALU.mult, op1=ALU.add).then_inc(x2_done, 1)
                    dve.wait_ge(x2_done, 2 * b + 2)
                    need(dve, ln2_small, 4 * b)
                    stats(b, st2, mv2, ln2_stat, bn_before(b, False))
                if exists(b - 1, B):
                    m = b - 1
                    need(dve, pt8_done, m + 1)
                    dve.tensor_copy(pr[:].rearrange("p c e -> p (c e)"), R_PROB).then_inc(top_step, 1)
                    dve.wait_ge(top_step, NTOP * m + 1)
                    wait_alone(dve, "dve")
                    for c in range(RC):
                        dve.max(top[:, c], pr[:, c]).then_inc(top_step, 1)
                    dve.wait_ge(top_step, NTOP * m + 3)
                    wait_alone(dve, "dve")
                    for c in range(RC):
                        dve.max_index(topi[:, c], top[:, c], pr[:, c]).then_inc(top_step, 1)
                    dve.wait_ge(top_step, NTOP * m + 5)
                    dve.tensor_copy(topf[:], topi[:, :, 0:TOPK]).then_inc(top_step, 1)
                    dve.wait_ge(top_step, NTOP * m + 6)
                    dve.tensor_tensor(oh[:].rearrange("p c k e -> p (c k) e"),
                                      topf[:].rearrange("p c k -> p (c k)").unsqueeze(2).broadcast_to([P, RC * TOPK, E]),
                                      iota_e[:].unsqueeze(1).broadcast_to([P, RC * TOPK, E]), ALU.is_equal
                                      ).then_inc(top_step, 1)
                    dve.wait_ge(top_step, NTOP * m + 7)
                    for r in range(2):
                        dve.tensor_tensor(ind2[:, :, r], oh[:, :, 0], oh[:, :, 1], ALU.add).then_inc(top_step, 1)

            def bn_before(m, first_norm):
                if first_norm:
                    seconds = m - 1 if not isinstance(m, int) else max(0, m - 1)
                    return RC * (m + seconds)
                firsts = m + 2 if not isinstance(m, int) else min(B, m + 2)
                return RC * (m + firsts)

            def wq_minus_mean(n):
                dve.wait_ge(s_wq_in[n], 16)
                dve.tensor_reduce(wq_mean[:, n, 0:1], wq_raw[:, n], AX_X, ALU.add).then_inc(s_wq_sum, 1)
                dve.wait_ge(s_wq_sum, n + 1)
                dve.tensor_scalar(wq_mean[:, n, 1:2], wq_mean[:, n, 0:1], -1.0 / D, None, ALU.mult).then_inc(s_wq_mean, 1)

            wq_minus_mean(0)
            for n in range(DC):
                if n + 1 < DC:
                    wq_minus_mean(n + 1)
                dve.wait_ge(s_wk_in[n], 16)
                dve.tensor_copy(wk_hi[:, n], wk_raw[:, n]).then_inc(s_wk_hi, 1)
                dve.wait_ge(s_wq_hi, n + 1)
                low(wq_lo[:, n], wq_raw[:, n], wq_hi[:, n], s_wq_lo)
                dve.wait_ge(s_wk_hi, n + 1)
                low(wk_lo[:, n], wk_raw[:, n], wk_hi[:, n], s_wk_lo)
            dve.wait_ge(s_wv_hi, 1)
            low(wv_lo[:], wv_raw[:], wv_hi[:], s_wv_lo)
            for n in range(DC):
                dve.wait_ge(a_his, n + 1)
                low(a_lo[:, n], bA[n][:], a_hi[:, n], a_los)
            dve.wait_ge(s_gw_hi, 1)
            low(gw_lo[:], gw_raw[:], gw_hi[:], s_gw_lo)
            dve.wait_ge(s_tanh, 2)
            pipeline(dve, batch, *BATCHES)

            step = [0]

            def link(ins):
                step[0] += 1
                ins.then_inc(table_step, 1)
                dve.wait_ge(table_step, step[0])

            dve.wait_ge(slot_step, NSTEP * B)
            link(dve.tensor_tensor(cnt[:], base[:, 0], ebase[:], ALU.subtract))
            link(dve.tensor_scalar(cnt_i[:, 0], cnt[:], float(TILE - 1), None, ALU.add))
            link(dve.tensor_scalar(cnt_i[:, 1], cnt_i[:, 0], 8, None, ALU.arith_shift_right))
            link(dve.tensor_copy(ntile[:], cnt_i[:, 1]))
            link(dve.tensor_tensor_scan(cum[:], onesE[:], ntile[:], 0.0, ALU.mult, ALU.add))
            link(dve.tensor_tensor(le[:], cum[:, 0:E - 1].unsqueeze(1).broadcast_to([P, NT, E - 1]),
                                   jidx[:].unsqueeze(2).broadcast_to([P, NT, E - 1]), ALU.is_le))
            link(dve.tensor_reduce(tile_e[:], le[:], AX_X, ALU.add))
            link(dve.tensor_tensor(lep[:], le[:], ntile[:, 0:E - 1].unsqueeze(1).broadcast_to([P, NT, E - 1]), ALU.mult))
            link(dve.tensor_reduce(tile_prev[:], lep[:], AX_X, ALU.add))
            link(dve.tensor_tensor(row1[:], jidx[:], tile_prev[:], ALU.subtract))
            link(dve.tensor_scalar(row2[:], row1[:], float(TILE), None, ALU.mult))
            link(dve.scalar_tensor_tensor(out=row3[:], in0=tile_e[:], scalar=float(REGION), in1=row2[:],
                                          op0=ALU.mult, op1=ALU.add))
            link(dve.tensor_scalar(extra[:], cum[:, E - 1:E], float(NT_MIN), None, ALU.subtract))
            link(dve.tensor_copy(table[:, :, 0], tile_e[:]))
            link(dve.tensor_copy(table[:, :, 1], row3[:]))
            dve.tensor_tensor(tile_onehot[:], tile_e[:].unsqueeze(1).broadcast_to([P, E, NT]),
                              iota_e[:].unsqueeze(2).broadcast_to([P, E, NT]), ALU.is_equal).then_inc(v_step, 1)
            dve.memset(vparts[:], 0.0).then_inc(v_step, 1)
            dve.wait_ge(v_step, 2)

            def split_w(n, m):
                dve.wait_ge(w_his[n], m + 1)
                low(w_lo[n][:], w_raw[n][:], w_hi[n][:], w_los[n])

            def h_high(n, m):
                need(dve, l_done[n + 1], 2 * m)
                for k in range(2):
                    dve.wait_ge(relu_done[n], DC * m + 2 * k + 2)
                    dve.tensor_copy(h_hi[n][:, 2 * k:2 * k + 2], h[n][:, 2 * k:2 * k + 2]).then_inc(h_his[n], 1)

            def tile(j, left):
                if has_tile(j, 0, left):
                    split_w(2, j)
                    h_high(1, j)
                if has_tile(j, 1, left):
                    split_w(1, j + 1)
                    h_high(0, j + 1)
                if has_tile(j, 2, left):
                    split_w(0, j + 2)
                    for k in range(2):
                        dve.wait_ge(et_his, 2 * (j + 2) + k + 1)
                        low(et_lo[:, 2 * k:2 * k + 2], two(bT[k]), et_hi[:, 2 * k:2 * k + 2], et_los)
                if has_tile(j, 0, left):
                    dve.wait_ge(b_in[2], 16 * (j + 1))
                    dve.wait_ge(wb_in, 16 * (j + 1))
                    dve.tensor_scalar(nb3[:], bias[2][:], -1.0, None, ALU.mult).then_inc(wsum_step, 1)
                    dve.tensor_reduce(wsum[:], wb[:], AX_X, ALU.add).then_inc(wsum_step, 1)
                    dve.wait_ge(wsum_step, 2 * j + 2)
                    for oc in range(DC):
                        if oc % 2 == 0:
                            dve.wait_ge(l_done[2], 2 * j + oc // 2 + 1)
                        z = bL[2][oc // 2][:, (oc % 2) * TILE:(oc % 2 + 1) * TILE]
                        dve.scalar_tensor_tensor(out=junk[:].rearrange("p (h t) -> p h t", h=TH),
                                                 in0=z.rearrange("p (h t) -> p h t", h=TH), scalar=nb3[:, oc:oc + 1],
                                                 in1=wb[:].rearrange("p (t h) -> p h t", h=TH),
                                                 op0=ALU.max, op1=ALU.mult,
                                                 accum_out=acc[:, oc:oc + 1]).then_inc(tail_small, 1)
                        dve.wait_ge(tail_small, DC * j + oc + 1)
                    dve.scalar_tensor_tensor(out=vparts[:, bass.ds(j, 1)].rearrange("p a c -> p (a c)"),
                                             in0=bias[2][:], scalar=wsum[:, 0:1], in1=acc[:],
                                             op0=ALU.mult, op1=ALU.add).then_inc(part_done, 1)

            tiles = tiles_in_use(dve)
            tile_pipeline(dve, tile, tiles)

            vstep = [2]

            def vlink(ins):
                vstep[0] += 1
                ins.then_inc(v_step, 1)
                dve.wait_ge(v_step, vstep[0])

            dve.wait_ge(part_done, tiles)
            for e in range(E):
                vstep[0] += 1
                dve.tensor_tensor(vprod[:, e], vparts[:].rearrange("p j c -> p c j"),
                                  tile_onehot[:, e].unsqueeze(1).broadcast_to([P, DC, NT]), ALU.mult).then_inc(v_step, 1)
            dve.wait_ge(v_step, vstep[0])
            vlink(dve.tensor_reduce(vt[:], vprod[:], AX_X, ALU.add))
            vlink(dve.tensor_scalar(vs[:], vt[:], tg_ffn[:, 0:1], None, ALU.mult))
            vlink(dve.tensor_copy(vs_hi[:], vs[:]))
            vlink(dve.tensor_copy(vhl[:, :, 0], vs_hi[:].bitcast(F32).rearrange("p e c -> p c e")))
            vlink(dve.tensor_tensor(vhl[:, :, 1], vs[:].rearrange("p e c -> p c e"),
                                    vs_hi[:].bitcast(F32).rearrange("p e c -> p c e"), ALU.subtract))
            dve.wait_ge(vt_done, 1)
            dve.tensor_copy(v16[:], bank[0][0:2 * E, :]).then_inc(v16_ready, 1)

            for n in range(B * RC):
                if n % 4 != 3:
                    dve.wait_ge(o_done, n + 1)
                    row = x_all[:, n // RC, n % RC]
                    dve.tensor_tensor(row, bank[n % 8][:], row, ALU.add).then_inc(res_dve, 1)

        @block.tensor
        def _(pe):
            def split_product(out_ap, left, right, done=None):
                n = len(left[0])
                for i in range(n):
                    lh, ll, rh, rl = left[0][i], left[1][i], right[0][i], right[1][i]
                    pe.matmul(out_ap, lh, rh, start=(i == 0), stop=False)
                    pe.matmul(out_ap, lh, rl, start=False, stop=False)
                    last = pe.matmul(out_ap, ll, rh, start=False, stop=(i == n - 1))
                if done is not None:
                    last.then_inc(done, 1)

            def cols(hi, lo, a, width):
                return ([hi[:, c, a:a + width] for c in range(hi.shape[1])],
                        [lo[:, c, a:a + width] for c in range(lo.shape[1])])

            def transpose_rows(src, banks, done):
                for dc in range(DC):
                    for c in range(RC):
                        last = pe.transpose(banks[dc // 2][:, (dc % 2) * S + c * P:(dc % 2) * S + (c + 1) * P],
                                            src[:, c, dc * P:(dc + 1) * P], ident[:])
                    if dc % 2 == 1:
                        last.then_inc(done, 1)

            for c in range(DC):
                pe.wait_ge(s_wq_lo, c + 1)
                pe.wait_ge(s_wk_lo, c + 1)
                for n in range(DC):
                    rows = slice(n * P, (n + 1) * P)
                    pe.matmul(bA[n][:], wq_hi[:, c, rows], wk_hi[:, c], start=(c == 0), stop=False)
                    pe.matmul(bA[n][:], wq_hi[:, c, rows], wk_lo[:, c], start=False, stop=False)
                    last = pe.matmul(bA[n][:], wq_lo[:, c, rows], wk_hi[:, c], start=False, stop=(c == DC - 1))
                    if c == DC - 1:
                        last.then_inc(a_mm, 1)
            pe.wait_ge(s_pool_const, 5)
            pe.wait_ge(s_wv_lo, 1)
            pe.wait_ge(s_gw_lo, 1)
            pe.wait_ge(a_los, DC)

            def batch(b):
                if exists(b, B):
                    need(pe, qa_los, 2 * (b + 1))
                    need(pe, c_los, b + 1)
                    need(pe, pt_los, b)
                    for c in range(RC):
                        split_product(bS[:, c * S:(c + 1) * S], cols(qa_hi, qa_lo, c * P, P), cols(c_hi, c_lo, 0, S),
                                      sc_done if c == RC - 1 else None)
                if exists(b, B):
                    need(pe, x2_done, 2 * b)
                    for c in range(RC):
                        split_product(bV[c][:], cols(c_hi, c_lo, c * P, P), cols(wv_hi, wv_lo, 0, D), v_done)
                if exists(b - 2, B):
                    need(pe, top_step, NTOP * (b - 1))
                    ind = ind2[:, :, 0]
                    pe.matmul(R_RANK, tri[:], ind, start=True, stop=True)
                    pe.matmul(R_TOT, ones[:], ind, start=True, stop=True)
                    for c in range(RC):
                        last = pe.transpose(bR[0:2 * E, c * P:(c + 1) * P],
                                            ind2[:, c].rearrange("p r e -> p (r e)"), ident[:])
                    last.then_inc(rank_done, 1)
                if exists(b, B):
                    need(pe, exp_done, RC * (b + 1))
                    for k in range(RC):
                        for c in range(RC):
                            last = pe.transpose(bS[:, k * S + c * P:k * S + (c + 1) * P],
                                                pexp[:, c, k * P:(k + 1) * P], ident[:])
                    last.then_inc(tp_done, 1)
                if exists(b - 1, B):
                    need(pe, xn2_ready, RC * b)
                    need(pe, gt_los, 2 * (b - 1))
                    transpose_rows(xn2, bG, tg_done)
                if exists(b + 1, B):
                    need(pe, xt_los, b + 2)
                    need(pe, qa_los, 2 * (b + 1))
                    for n in range(DC):
                        split_product(bQ[n // 2][:, (n % 2) * S:(n % 2 + 1) * S], cols(a_hi, a_lo, n * P, P),
                                      cols(xt_hi, xt_lo, 0, S), qa_done if n % 2 == 1 else None)
                if exists(b - 1, B):
                    need(pe, gt_los, 2 * b)
                    need(pe, slot_step, NSTEP * (b - 2) + 4)
                    split_product(R_LOGIT, cols(gw_hi, gw_lo, 0, E), cols(gt_hi, gt_lo, 0, S), gate_done)
                if exists(b, B):
                    need(pe, pt_los, b + 1)
                    need(pe, v_los, 2 * (b + 1))
                    for c in range(RC):
                        split_product(bV[c][:], cols(pt_hi, pt_lo, c * P, P), cols(v_hi, v_lo, 0, D), pv_done)
                if exists(b - 1, B):
                    need(pe, probs_ready, b)
                    wait_alone(pe, "pe")
                    for c in range(RC):
                        last = pe.transpose(R_PROB[:, c * E:(c + 1) * E], probs[:, c * P:(c + 1) * P],
                                            ident[0:E, 0:E])
                    last.then_inc(pt8_done, 1)

            pipeline(pe, batch, *BATCHES)

            def layer(n, m, src_hi, src_lo):
                for oc in range(DC):
                    split_product(bL[n][oc // 2][:, (oc % 2) * TILE:(oc % 2 + 1) * TILE],
                                  cols(w_hi[n], w_lo[n], oc * P, P), cols(src_hi, src_lo, 0, TILE),
                                  l_done[n] if oc % 2 == 1 else None)

            def tile(j, left):
                if has_tile(j, 0, left):
                    need(pe, w_los[1], j + 1)
                    need(pe, h_los[0], 2 * (j + 1))
                    need(pe, relu_done[1], DC * j)
                    layer(1, j, h_hi[0], h_lo[0])
                if has_tile(j, 1, left):
                    need(pe, w_los[0], j + 2)
                    need(pe, et_los, 2 * (j + 2))
                    need(pe, relu_done[0], DC * (j + 1))
                    layer(0, j + 1, et_hi, et_lo)
                if has_tile(j, 2, left):
                    need(pe, gathered, 16 * TH * (j + 3))
                    need(pe, et_los, 2 * (j + 2))
                    transpose_rows(xg, bT, te_done)
                if has_tile(j, 0, left):
                    need(pe, w_los[2], j + 1)
                    need(pe, h_los[1], 2 * (j + 1))
                    need(pe, part_done, j)
                    layer(2, j, h_hi[1], h_lo[1])

            tile_pipeline(pe, tile, tiles_in_use(pe))

            pe.wait_ge(v_step, 2 + E + 5)
            for c in range(DC):
                last = pe.transpose(bank[0][0:2 * E, c * P:(c + 1) * P],
                                    vhl[:, c].rearrange("p r e -> p (r e)"), ident[:])
            last.then_inc(vt_done, 1)
            pe.wait_ge(v16_ready, 1)
            for n in range(B * RC):
                if n >= 8 and n % 4 == 3:
                    pe.wait_ge(res_copied, (n - 8) // 4 + 1)
                elif n >= 8:
                    pe.wait_ge(res_dve, n - 7 - (n - 7) // 4)
                pe.matmul(bank[n % 8][:], ind16[:, n * P:(n + 1) * P], v16[:], start=True, stop=True
                          ).then_inc(o_done, 1)


def _chunks(a):
    lead = a.shape[:-2]
    a = a.reshape(*lead, a.shape[-2] // P, P, a.shape[-1])
    return np.ascontiguousarray(np.swapaxes(a, -3, -2))


def kernel(x, ctx_1024, g_xattn, g_ffn, L0_xattn_Wq, L0_xattn_Wkv, L0_ffn_gate_w, L0_ffn_gate_b,
           L0_ffn_w1, L0_ffn_b1, L0_ffn_w2, L0_ffn_b2, L0_ffn_w3, L0_ffn_b3):
    import concourse.bacc as _bacc
    from concourse.bass_utils import run_bass_kernel_spmd as _run

    wkv = np.asarray(L0_xattn_Wkv)
    arrays = {
        "x": np.ascontiguousarray(x),
        "x_t": _chunks(np.swapaxes(np.asarray(x), 1, 2)),
        "ctx_t": _chunks(np.swapaxes(np.asarray(ctx_1024), 1, 2)),
        "g_xattn": np.ascontiguousarray(g_xattn),
        "g_ffn": np.ascontiguousarray(g_ffn),
        "wq_t": _chunks(np.asarray(L0_xattn_Wq).T),
        "wk_t": _chunks(wkv[:, :D].T),
        "wv": _chunks(wkv[:, D:]),
        "gate_w": _chunks(np.asarray(L0_ffn_gate_w)),
        "gate_b": np.ascontiguousarray(L0_ffn_gate_b),
        "w1": _chunks(np.asarray(L0_ffn_w1)),
        "w2": _chunks(np.asarray(L0_ffn_w2)),
        "w3": _chunks(np.asarray(L0_ffn_w3)),
        "b1": np.ascontiguousarray(np.swapaxes(np.asarray(L0_ffn_b1).reshape(E, DC, P), 1, 2)),
        "b2": np.ascontiguousarray(np.swapaxes(np.asarray(L0_ffn_b2).reshape(E, DC, P), 1, 2)),
        "b3": np.ascontiguousarray(np.swapaxes(np.asarray(L0_ffn_b3).reshape(E, DC, P), 1, 2)),
    }
    nc = _bacc.Bacc("TRN2", target_bir_lowering=False, num_devices=1)
    args = [nc.dram_tensor(f"in_{k}", a.shape, F32, kind="ExternalInput").ap() for k, a in arrays.items()]
    out = nc.dram_tensor("out", (B, S, D), F32, kind="ExternalOutput").ap()
    xn2_dram = nc.dram_tensor("xn2_dram", (TOK, D), F32).ap()
    slot_tok = nc.dram_tensor("slot_tok", (NSLOT, 1), U32).ap()
    slot_w = nc.dram_tensor("slot_w", (NSLOT, 1), F32).ap()
    flamingo_block(nc, *args, out, xn2_dram, slot_tok, slot_w)
    r = _run(nc, [{f"in_{k}": a for k, a in arrays.items()}], core_ids=[0])
    return r.results[0]["out"]
```

```python
from contextlib import ExitStack

import numpy as np
import concourse.bass as bass
from concourse import mybir

F32 = mybir.dt.float32
F32R = mybir.dt.float32r
I32 = mybir.dt.int32
U32 = mybir.dt.uint32
BF16 = mybir.dt.bfloat16
ALU = mybir.AluOpType
ACT = mybir.ActivationFunctionType
AX_X = mybir.AxisListType.X

P = 128
B, S, D, E = 16, 256, 512, 8
TOK = B * S
TOPK = 2
DC = D // P
RC = S // P
TILE = 256
TH = TILE // P
EXPERTS_OWN = (DC * D + 6 * DC * TILE) * 4 + 256
NT_MIN = TOK * TOPK // TILE
NT = NT_MIN + E - 1
TILE_SHIFT = TILE.bit_length() - 1
REGION = TOK
NSLOT = E * REGION
GLO = 32
EPS = 1e-5
SCALE = 1.0 / float(np.sqrt(D))


def need(eng, sem, value):
    if not isinstance(value, int) or value > 0:
        eng.wait_ge(sem, value)


def exists(m, count):
    return not isinstance(m, int) or 0 <= m < count


def pipeline(eng, body, first, loop_first, loop_end, end):
    for i in range(first, loop_first):
        body(i)
    with eng.Fori(loop_first, loop_end) as i:
        body(i)
    for i in range(loop_end, end):
        body(i)


BATCHES = (-1, 3, B - 3, B - 1)

AHEAD = 4

KNOWN = B - 4
EARLY = 8
assert EARLY <= (KNOWN * S * TOPK - E * (TILE - 1)) // TILE and EARLY >= AHEAD + 2


def tile_pipeline(eng, body, tiles):
    with eng.Fori(2, tiles - AHEAD) as j:
        body(j, AHEAD + 1)
    for left in range(AHEAD, 0, -1):
        body(tiles - left, left)


def has_tile(ahead, left):
    return ahead < left


def flamingo_block(nc, x, x_t, ctx_t, g_xattn, g_ffn, wq_t, wk_t, wv, gate_w, gate_b,
                   w1, w2, w3, b1, b2, b3, out, xn2_dram, slot_tok, slot_w):
    x_v = x.rearrange("b (c p) d -> b p c d", p=P)
    out_v = out.rearrange("b (c p) d -> b p c d", p=P)
    xn2_v = xn2_dram.rearrange("(b c p) d -> b p c d", c=RC, p=P)
    w_dram = [w1, w2, w3]
    b_dram = [b1, b2, b3]

    with ExitStack() as ctx:
        def sem(name):
            return ctx.enter_context(nc.semaphore(name))

        def alloc(stack, name, shape, dt):
            return stack.enter_context(nc.sbuf_tensor(name, shape, dt))

        ident = alloc(ctx, "ident", [P, P], F32)
        tri = alloc(ctx, "tri", [P, P], F32)
        ones = alloc(ctx, "ones", [P, P], F32)
        tg_attn = alloc(ctx, "tg_attn", [P, 1], F32)
        tg_ffn = alloc(ctx, "tg_ffn", [P, 1], F32)
        g_raw = alloc(ctx, "g_raw", [P, 2], F32)
        wq_mean = alloc(ctx, "wq_mean", [P, DC, 2], F32)
        iota_i = alloc(ctx, "iota_i", [P, E], I32)
        ebase_i = alloc(ctx, "ebase_i", [P, E], I32)
        jidx_i = alloc(ctx, "jidx_i", [P, NT], I32)
        iota_e = alloc(ctx, "iota_e", [P, E], F32)
        ebase = alloc(ctx, "ebase", [P, E], F32)
        jidx = alloc(ctx, "jidx", [P, NT], F32)
        tokall = alloc(ctx, "tokall", [P, B * RC], U32)
        base = alloc(ctx, "base", [P, RC, E], F32)
        table = alloc(ctx, "table", [P, NT, 2], I32)
        extra = alloc(ctx, "extra", [P, 1], I32)
        tile_onehot = alloc(ctx, "tile_onehot", [P, E, NT], F32)
        part = alloc(ctx, "part", [P, DC], F32)
        v_add = alloc(ctx, "v_add", [P, E, DC], F32)
        v_sum = alloc(ctx, "v_sum", [P, E, DC], F32)
        ind24 = alloc(ctx, "ind24", [3 * E, TOK], BF16)

        with ExitStack() as tmp:
            alloc(tmp, "x_head_room", [P, 2 * RC * D], F32)
            wq_raw = alloc(tmp, "wq_raw", [P, DC, D], F32)
            wk_raw = alloc(tmp, "wk_raw", [P, DC, D], F32)
            wv_raw = alloc(tmp, "wv_raw", [P, DC, D], F32)
            wq_hi = alloc(tmp, "wq_hi", [P, DC, D], F32R)
            wq_lo = alloc(tmp, "wq_lo", [P, DC, D], F32R)
            wk_hi = alloc(tmp, "wk_hi", [P, DC, D], F32R)
            wk_lo = alloc(tmp, "wk_lo", [P, DC, D], F32R)
        x_all = alloc(ctx, "x_all", [P, B, RC, D], F32)

        with ExitStack() as ph:
            a_hi = alloc(ph, "a_hi", [P, DC, D], F32R)
            a_lo = alloc(ph, "a_lo", [P, DC, D], F32R)
            wv_hi = alloc(ph, "wv_hi", [P, DC, D], F32R)
            wv_lo = alloc(ph, "wv_lo", [P, DC, D], F32R)
            c_raw = alloc(ph, "c_raw", [P, DC, S], F32)
            c_hi = alloc(ph, "c_hi", [P, DC, S], F32R)
            c_lo = alloc(ph, "c_lo", [P, DC, S], F32R)
            qa_hi = alloc(ph, "qa_hi", [P, DC, S], F32R)
            qa_lo = alloc(ph, "qa_lo", [P, DC, S], F32R)
            v_hi = alloc(ph, "v_hi", [P, RC, D], F32R)
            v_lo = alloc(ph, "v_lo", [P, RC, D], F32R)
            pexp = alloc(ph, "pexp", [P, RC, S], F32)
            pt_hi = alloc(ph, "pt_hi", [P, RC, S], F32R)
            pt_lo = alloc(ph, "pt_lo", [P, RC, S], F32R)
            xt_raw = alloc(ph, "xt_raw", [P, DC, S], F32)
            xt_hi = alloc(ph, "xt_hi", [P, DC, S], F32R)
            xt_lo = alloc(ph, "xt_lo", [P, DC, S], F32R)
            zeros = alloc(ph, "zeros", [P, NSLOT // P], F32)
            alloc(ph, "experts_own_room", [P, EXPERTS_OWN // 4 - NSLOT // P], F32)
            gw_raw = alloc(ph, "gw_raw", [P, DC, E], F32)
            gw = alloc(ph, "gw", [P, DC, GLO + E], F32R)
            gb = alloc(ph, "gb", [E, 1], F32)
            st1 = alloc(ph, "st1", [P, RC, 6], F32)
            mv1 = alloc(ph, "mv1", [P, RC, 2], F32)
            rn1 = alloc(ph, "rn1", [P, 4, RC], F32)
            st2 = alloc(ph, "st2", [P, RC, 6], F32)
            mv2 = alloc(ph, "mv2", [P, RC, 2], F32)
            rn2 = alloc(ph, "rn2", [P, 4, RC], F32)
            mhalf = alloc(ph, "mhalf", [P, RC], F32)
            smax = alloc(ph, "smax", [P, RC], F32)
            nbias = alloc(ph, "nbias", [P, RC], F32)
            ssum = alloc(ph, "ssum", [P, RC], F32)
            rsum = alloc(ph, "rsum", [P, RC], F32)
            coef = alloc(ph, "coef", [P, RC], F32)
            logit_low = alloc(ph, "logit_low", [E, S], F32)
            logit = alloc(ph, "logit", [E, S], F32)
            gmax = alloc(ph, "gmax", [E, 2], F32)
            gexp = alloc(ph, "gexp", [E, S], F32)
            gsum = alloc(ph, "gsum", [E, 2], F32)
            probs = alloc(ph, "probs", [E, S], F32)
            pr = alloc(ph, "pr", [P, RC, E], F32)
            top = alloc(ph, "top", [P, RC, E], F32)
            topi = alloc(ph, "topi", [P, RC, E], U32)
            topf = alloc(ph, "topf", [P, RC, TOPK], F32)
            oh = alloc(ph, "oh", [P, RC, TOPK, E], F32)
            ind3 = alloc(ph, "ind3", [P, RC, 3, E], F32)
            full = alloc(ph, "full", [P, RC, E], F32)
            prod = alloc(ph, "prod", [P, RC, TOPK, E], F32)
            pos = alloc(ph, "pos", [P, RC, TOPK], F32)
            slot_u = alloc(ph, "slot_u", [P, B - KNOWN, RC * TOPK], U32)
            tok_u = alloc(ph, "tok_u", [P, B - KNOWN, RC], U32)
            w_out = alloc(ph, "w_out", [P, B - KNOWN, RC * TOPK], F32)
            cnt = alloc(ph, "cnt", [P, E], F32)
            cnt_i = alloc(ph, "cnt_i", [P, 2, E], I32)
            ntile = alloc(ph, "ntile", [P, E], F32)
            cum = alloc(ph, "cum", [P, E], F32)
            onesE = alloc(ph, "onesE", [P, E], F32)
            le = alloc(ph, "le", [P, NT, E - 1], F32)
            lep = alloc(ph, "lep", [P, NT, E - 1], F32)
            tile_e = alloc(ph, "tile_e", [P, NT], F32)
            tile_prev = alloc(ph, "tile_prev", [P, NT], F32)
            row1 = alloc(ph, "row1", [P, NT], F32)
            row2 = alloc(ph, "row2", [P, NT], F32)
            row3 = alloc(ph, "row3", [P, NT], F32)
            before = alloc(ph, "before", [P, E], F32)
            ntile_all = alloc(ph, "ntile_all", [P, E], F32)
            passed = alloc(ph, "passed", [P, E - 1], F32)
            xn2 = alloc(ph, "xn2", [P, RC, D], F32)
            gt_hi = alloc(ph, "gt_hi", [P, DC, S], F32R)
            gt_lo = alloc(ph, "gt_lo", [P, DC, S], F32R)

        with ExitStack() as ph:
            w_raw = [alloc(ph, f"w_raw{n}", [P, DC, D], F32) for n in range(2)]
            w_hi0 = alloc(ph, "w_hi0", [P, DC, D], F32R)
            w_lo0 = alloc(ph, "w_lo0", [P, DC, D], F32R)
            w_raw.append(alloc(ph, "w_raw2", [P, DC, D], F32))
            w_hi1 = alloc(ph, "w_hi1", [P, DC, D], F32R)
            w_hi2 = alloc(ph, "w_hi2", [P, DC, D], F32R)
            w_lo2 = alloc(ph, "w_lo2", [P, DC, D], F32R)
            wb = alloc(ph, "wb", [P, TILE], F32)
            junk = alloc(ph, "junk", [P, TILE], F32)
            xg = alloc(ph, "xg", [P, TH, D], F32)
            et_hi = alloc(ph, "et_hi", [P, DC, TILE], F32R)
            et_lo = alloc(ph, "et_lo", [P, DC, TILE], F32R)
            w_lo1 = alloc(ph, "w_lo1", [P, DC, D], F32R)
            h = [alloc(ph, f"h{n}", [P, DC, TILE], F32) for n in range(2)]
            h_hi = [alloc(ph, f"h_hi{n}", [P, DC, TILE], F32R) for n in range(2)]
            h_lo = [alloc(ph, f"h_lo{n}", [P, DC, TILE], F32R) for n in range(2)]
            bias = [alloc(ph, f"bias{n}", [P, DC], F32) for n in range(3)]
            idx = alloc(ph, "idx", [P, TH], U32)
            nb3 = alloc(ph, "nb3", [P, DC], F32)
            wsum = alloc(ph, "wsum", [P, 1], F32)
            acc = alloc(ph, "acc", [P, DC], F32)
            w_hi, w_lo = [w_hi0, w_hi1, w_hi2], [w_lo0, w_lo1, w_lo2]

        with ExitStack() as ph:
            vs = alloc(ph, "vs", [P, E, DC], F32)
            vs_part = alloc(ph, "vs_part", [P, 2, E, DC], BF16)
            vs_rest = alloc(ph, "vs_rest", [P, E, DC], F32)
            v3 = alloc(ph, "v3", [P, DC, 3, E], F32)
            v_rows = alloc(ph, "v_rows", [P, 2, D], F32)
            v24 = alloc(ph, "v24", [3 * E, D], BF16)

        bank = [ctx.enter_context(nc.psum_tensor(f"bank{n}", [P, 512], F32)) for n in range(8)]
        bS = bank[0]
        bQ = [bank[1], bank[2]]
        bV = [bank[3], bank[4]]
        bG = [bank[5], bank[6]]
        bR = bank[7]
        bA = [bank[3], bank[4], bank[5], bank[6]]
        bL = [[bank[0], bank[3]], [bank[4], bank[5]], [bank[6], bank[7]]]
        bZ = [bank[6], bank[7], bank[0], bank[3]]
        bT = [bank[1], bank[2]]
        R_LOGIT = bR[0:E, 0:S]
        R_LOGIT_LOW = bR[GLO:GLO + E, 0:S]
        R_IND = bR[0:3 * E, 0:S]
        R_PROB = bR[:, 256:256 + RC * E]
        R_RANK = bR[:, 288:288 + RC * E]
        R_TOT = bR[:, 304:304 + RC * E]

        s_iota = sem("s_iota")
        s_pool_const = sem("s_pool_const")
        s_conv = sem("s_conv")
        s_zero = sem("s_zero")
        s_zero_dma = sem("s_zero_dma")
        s_small = sem("s_small")
        s_tanh = sem("s_tanh")
        s_wq_in = [sem(f"s_wq_in{n}") for n in range(DC)]
        s_wk_in = [sem(f"s_wk_in{n}") for n in range(DC)]
        s_wv_in = sem("s_wv_in")
        s_wq_hi, s_wk_hi, s_wv_hi, s_gw_hi = sem("s_wq_hi"), sem("s_wk_hi"), sem("s_wv_hi"), sem("s_gw_hi")
        s_wq_lo, s_wk_lo, s_wv_lo, s_gw_lo = sem("s_wq_lo"), sem("s_wk_lo"), sem("s_wv_lo"), sem("s_gw_lo")
        a_mm, a_his, a_los = sem("a_mm"), sem("a_his"), sem("a_los")
        x_in, c_in = sem("x_in"), sem("c_in")
        ln1_stat, ln1_small, xt_in = sem("ln1_stat"), sem("ln1_small"), sem("xt_in")
        s_gw_zero = sem("s_gw_zero")
        s_wq_sum, s_wq_mean, s_wq_c = sem("s_wq_sum"), sem("s_wq_mean"), sem("s_wq_c")
        ln2_stat, ln2_small, xn2_ready = sem("ln2_stat"), sem("ln2_small"), sem("xn2_ready")
        c_his, c_los = sem("c_his"), sem("c_los")
        xt_his, xt_los = sem("xt_his"), sem("xt_los")
        qa_done, qa_his, qa_los = sem("qa_done"), sem("qa_his"), sem("qa_los")
        sc_done, nbias_ready, exp_done = sem("sc_done"), sem("nbias_ready"), sem("exp_done")
        tp_done, pt_his, pt_los = sem("tp_done"), sem("pt_his"), sem("pt_los")
        v_done, v_his, v_los = sem("v_done"), sem("v_his"), sem("v_los")
        pv_done, coef_ready, x2_done, xn2_out = sem("pv_done"), sem("coef_ready"), sem("x2_done"), sem("xn2_out")
        tg_done, gt_his, gt_los = sem("tg_done"), sem("gt_his"), sem("gt_los")
        gate_done, gmax_ready, gexp_done, probs_ready = sem("gate_done"), sem("gmax_ready"), sem("gexp_done"), sem("probs_ready")
        pt8_done, top_step, rank_done, slot_step = sem("pt8_done"), sem("top_step"), sem("rank_done"), sem("slot_step")
        tok_sent, w_sent = sem("tok_sent"), sem("w_sent")
        v_acc = sem("v_acc")
        early_step, table_step = sem("early_step"), sem("table_step")
        w_in = [sem(f"w_in{n}") for n in range(3)]
        b_in = [sem(f"b_in{n}") for n in range(3)]
        w_his = [sem(f"w_his{n}") for n in range(3)]
        w_los = [sem(f"w_los{n}") for n in range(3)]
        idx_in, wb_in, gathered = sem("idx_in"), sem("wb_in"), sem("gathered")
        te_done, et_his, et_los = sem("te_done"), sem("et_his"), sem("et_los")
        l_done = [sem(f"l_done{n}") for n in range(3)]
        relu_done = [sem(f"relu_done{n}") for n in range(2)]
        h_his = [sem(f"h_his{n}") for n in range(2)]
        h_los = [sem(f"h_los{n}") for n in range(2)]
        bn_step, gate_step = sem("bn_step"), sem("gate_step")
        tail_small, wsum_step, part_done = sem("tail_small"), sem("wsum_step"), sem("part_done")
        v_step, vt_done, v24_ready = sem("v_step"), sem("vt_done"), sem("v24_ready")
        o_done, out_sent = sem("o_done"), sem("out_sent")
        res_dve, res_copied, res_pool = sem("res_dve"), sem("res_copied"), sem("res_pool")

        NTOP, NSTEP = 10, 9
        NEARLY, NTAB = 15, 20

        waited = {name: sem(f"waited_{name}") for name in ("sp", "act", "pool", "dve", "pe")}

        def buf(m):
            return m - KNOWN if isinstance(m, int) and m > KNOWN else 0

        def wait_alone(eng, name):
            eng.sem_inc(waited[name], 1)

        def tiles_in_use(eng):
            eng.wait_ge(table_step, NTAB)
            return eng.value_load(extra[0:1, 0:1], min_val=0, max_val=NT - NT_MIN) + NT_MIN

        block = ctx.enter_context(nc.Block())

        @block.sync
        def _(sp):
            for n in range(DC):
                sp.dma_start(wq_raw[:, n], wq_t[:, n]).then_inc(s_wq_in[n], 16)
                sp.dma_start(wk_raw[:, n], wk_t[:, n]).then_inc(s_wk_in[n], 16)
            sp.dma_start(xt_raw[:], x_t[0]).then_inc(xt_in, 16)
            sp.dma_start(g_raw[:, 0:1], g_xattn.rearrange("(a n) -> a n", a=1).broadcast_to([P, 1])).then_inc(s_small, 16)
            sp.dma_start(g_raw[:, 1:2], g_ffn.rearrange("(a n) -> a n", a=1).broadcast_to([P, 1])).then_inc(s_small, 16)
            sp.dma_start(gw_raw[:], gate_w).then_inc(s_small, 16)
            sp.dma_start(gb[:], gate_b.rearrange("(e n) -> e n", n=1)).then_inc(s_small, 16)
            sp.dma_start(x_all[:, 0], x_v[0]).then_inc(x_in, 16)
            sp.dma_start(wv_raw[:], wv).then_inc(s_wv_in, 16)
            sp.wait_ge(s_zero, 1)
            sp.dma_start(slot_tok.rearrange("(p n) a -> p (n a)", p=P), zeros[:].bitcast(U32)).then_inc(s_zero_dma, 16)
            sp.dma_start(slot_w.rearrange("(p n) a -> p (n a)", p=P), zeros[:]).then_inc(s_zero_dma, 16)

            def store_xn2(m):
                need(sp, xn2_ready, RC * (m + 1))
                sp.dma_start(xn2_v[bass.ds(m, 1)].rearrange("a p c d -> p a c d"),
                             xn2[:].rearrange("p (a c) d -> p a c d", a=1)).then_inc(xn2_out, 16)

            def batch(b):
                if exists(b + 1, B):
                    need(sp, c_los, b + 1)
                    sp.dma_start(c_raw[:], ctx_t[b + 1] if isinstance(b, int) else
                                 ctx_t[bass.ds(b + 1, 1)].rearrange("a p c s -> (a p) c s")).then_inc(c_in, 16)
                if exists(b + 3, B):
                    need(sp, x_in, (b + 3) * 16)
                    if isinstance(b, int) and b + 3 == 2:
                        sp.wait_ge(a_mm, DC)
                        sp.wait_ge(s_wv_lo, 1)
                    sp.dma_start(x_all[:, bass.ds(b + 3, 1)], x_v[bass.ds(b + 3, 1)].rearrange("a p c d -> p a c d")
                                 ).then_inc(x_in, 16)
                if exists(b - 1, B):
                    store_xn2(b - 1)
                if exists(b + 2, B) and not (isinstance(b, int) and b + 2 == 0):
                    need(sp, xt_los, b + 2)
                    sp.dma_start(xt_raw[:], x_t[b + 2] if isinstance(b, int) else
                                 x_t[bass.ds(b + 2, 1)].rearrange("a p c s -> (a p) c s")).then_inc(xt_in, 16)

            batch(-2)
            pipeline(sp, batch, *BATCHES)

            def load_w(n, m):
                need(sp, w_los[n], m)
                wait_alone(sp, "sp")
                e = sp.value_load(table[0:1, bass.ds(m, 1), 0:1], min_val=0, max_val=E - 1)

                def load():
                    sp.dma_start(w_raw[n][:], w_dram[n][bass.ds(e, 1)].rearrange("a p c d -> (a p) c d")
                                 ).then_inc(w_in[n], 16)

                if isinstance(m, int) and m == 0:
                    load()
                    return
                previous = sp.value_load(table[0:1, bass.ds(m - 1, 1), 0:1], min_val=0, max_val=E - 1)
                with sp.If(e != previous):
                    load()
                with sp.Else():
                    sp.sem_inc(w_in[n], 16)

            def load_b(n, m):
                if n < 2:
                    need(sp, relu_done[n], DC * m)
                else:
                    need(sp, part_done, m)
                wait_alone(sp, "sp")
                e = sp.value_load(table[0:1, bass.ds(m, 1), 0:1], min_val=0, max_val=E - 1)
                sp.dma_start(bias[n][:], b_dram[n][bass.ds(e, 1)].rearrange("a p c -> (a p) c")
                             ).then_inc(b_in[n], 16)

            def load_idx(m):
                need(sp, gathered, 16 * TH * m)
                wait_alone(sp, "sp")
                r = sp.value_load(table[0:1, bass.ds(m, 1), 1:2], min_val=0, max_val=NSLOT - TILE)
                sp.dma_start(idx[:], slot_tok[bass.ds(r, TILE)].rearrange("(p h) a -> p (h a)", p=P)
                             ).then_inc(idx_in, 16)

            def load_wb(m):
                need(sp, part_done, m)
                wait_alone(sp, "sp")
                r = sp.value_load(table[0:1, bass.ds(m, 1), 1:2], min_val=0, max_val=NSLOT - TILE)
                sp.dma_start(wb[:], slot_w[bass.ds(r, TILE)].rearrange("n a -> a n").broadcast_to([P, TILE])
                             ).then_inc(wb_in, 16)

            sp.wait_ge(early_step, NEARLY)
            sp.wait_ge(tok_sent, 16 * RC * TOPK * KNOWN)
            load_idx(0)
            sp.wait_ge(qa_done, 2 * B)
            load_w(0, 0)
            load_w(1, 0)
            for n in range(3):
                load_b(n, 0)
            load_idx(1)
            store_xn2(B - 2)
            sp.wait_ge(c_los, B)
            sp.wait_ge(v_done, RC * B)
            load_w(2, 0)
            load_w(0, 1)
            load_idx(2)
            store_xn2(B - 1)
            sp.wait_ge(slot_step, NSTEP * KNOWN + 7)
            sp.wait_ge(pv_done, RC * B)
            load_wb(0)
            load_w(1, 1)
            load_b(0, 1)
            load_w(0, 2)
            load_idx(3)

            def tile(j, left):
                if has_tile(1, left):
                    load_w(2, j + 1)
                    load_b(1, j + 1)
                if has_tile(2, left):
                    load_w(1, j + 2)
                    load_b(0, j + 2)
                if has_tile(3, left):
                    load_w(0, j + 3)
                if has_tile(1, left):
                    load_b(2, j + 1)
                    load_wb(j + 1)
                if has_tile(4, left):
                    load_idx(j + 4)

            tile(0, AHEAD + 1)
            tile(1, AHEAD + 1)
            tiles = tiles_in_use(sp)
            sp.wait_ge(tok_sent, 16 * RC * TOPK * B)
            sp.wait_ge(w_sent, 16 * RC * TOPK * B)
            tile_pipeline(sp, tile, tiles)

            for b in range(B):
                sp.wait_ge(res_dve, RC * (b + 1) - (b + 1) // 2)
                if b % 2 == 1:
                    sp.wait_ge(res_pool, (b + 1) // 2)
                sp.dma_start(out_v[b], x_all[:, b]).then_inc(out_sent, 16)
            sp.wait_ge(out_sent, 16 * B)

        @block.gpsimd
        def _(pool):
            pool.memset(zeros[:], 0.0).then_inc(s_zero, 1)
            pool.memset(ident[:], 0.0).then_inc(s_iota, 1)
            pool.memset(ones[:], 1.0).then_inc(s_pool_const, 1)
            pool.memset(tri[:], 1.0).then_inc(s_iota, 1)
            pool.memset(mhalf[:], -0.5).then_inc(s_pool_const, 1)
            pool.memset(onesE[:], 1.0).then_inc(s_pool_const, 1)
            pool.wait_ge(s_iota, 2)
            pool.affine_select(out=ident[:], in_=ident[:], compare_op=ALU.not_equal, fill=1.0, base=0,
                               pattern=[[-1, P]], channel_multiplier=1).then_inc(s_pool_const, 1)
            pool.affine_select(out=tri[:], in_=tri[:], compare_op=ALU.is_gt, fill=0.0, base=0,
                               pattern=[[1, P]], channel_multiplier=-1).then_inc(s_pool_const, 1)
            pool.iota(iota_i[:], pattern=[[1, E]], base=0, channel_multiplier=0).then_inc(s_iota, 1)
            pool.iota(ebase_i[:], pattern=[[REGION, E]], base=0, channel_multiplier=0).then_inc(s_iota, 1)
            pool.iota(jidx_i[:], pattern=[[1, NT]], base=0, channel_multiplier=0).then_inc(s_iota, 1)
            pool.iota(tokall[:], pattern=[[P, B * RC]], base=0, channel_multiplier=1).then_inc(s_iota, 1)
            pool.wait_ge(s_pool_const, 5)

            def inverse_deviation(mv, rn, done, m):
                wait_alone(pool, "pool")
                pool.tensor_scalar(rn[:, 0, :], mv[:, :, 1], EPS, None, ALU.add).then_inc(done, 1)
                pool.wait_ge(done, 4 * m + 1)
                pool.tensor_tensor(rn[:, 1, :], rn[:, 0, :], mhalf[:], ALU.pow).then_inc(done, 1)
                pool.wait_ge(done, 4 * m + 2)
                wait_alone(pool, "pool")

            def norm1_scale(m):
                need(pool, ln1_stat, RC * (m + 1))
                need(pool, exp_done, RC * m)
                inverse_deviation(mv1, rn1, ln1_small, m)
                pool.tensor_scalar(rn1[:, 2, :], rn1[:, 1, :], SCALE, None, ALU.mult).then_inc(ln1_small, 1)
                pool.tensor_scalar(rn1[:, 3, :], rn1[:, 1, :], -SCALE, None, ALU.mult).then_inc(ln1_small, 1)

            def norm2_scale(m):
                need(pool, ln2_stat, RC * (m + 1))
                need(pool, xn2_ready, RC * m)
                inverse_deviation(mv2, rn2, ln2_small, m)
                pool.tensor_scalar(rn2[:, 2, :], mv2[:, :, 0], -1.0, None, ALU.mult).then_inc(ln2_small, 1)
                pool.wait_ge(ln2_small, 4 * m + 3)
                pool.tensor_tensor(rn2[:, 3, :], rn2[:, 2, :], rn2[:, 1, :], ALU.mult).then_inc(ln2_small, 1)

            def context_low(m):
                need(pool, c_his, m + 1)
                pool.tensor_tensor(c_lo[:], c_raw[:], c_hi[:].bitcast(F32), ALU.subtract).then_inc(c_los, 1)

            def send_tokens(m):
                need(pool, slot_step, NSTEP * (m + 1))
                if isinstance(m, int) and m == 0:
                    pool.wait_ge(s_zero_dma, 32)
                wait_alone(pool, "pool")
                for n in range(RC * TOPK):
                    pool.indirect_dma_start(slot_tok, bass.IndirectOffsetOnAxis(ap=slot_u[:, buf(m), n:n + 1], axis=0),
                                            tok_u[:, buf(m), n // TOPK:n // TOPK + 1], None).then_inc(tok_sent, 16)

            def send_weights(m):
                for n in range(RC * TOPK):
                    pool.indirect_dma_start(slot_w, bass.IndirectOffsetOnAxis(ap=slot_u[:, buf(m), n:n + 1], axis=0),
                                            w_out[:, buf(m), n:n + 1], None).then_inc(w_sent, 16)

            def batch(b):
                if isinstance(b, int) and b == BATCHES[0]:
                    context_low(0)
                    norm1_scale(0)
                elif exists(b + 1, B):
                    norm1_scale(b + 1)
                    context_low(b + 1)
                if isinstance(b, int) and b == KNOWN + 2:
                    gather(0)
                if exists(b - 2, B):
                    send_tokens(b - 2)
                    send_weights(b - 2)
                if exists(b, B):
                    norm2_scale(b)

            def gather(m):
                need(pool, idx_in, 16 * (m + 1))
                if isinstance(m, int) and m == 0:
                    pool.wait_ge(xn2_ready, RC * KNOWN + 1)
                    pool.wait_ge(xt_los, B)
                need(pool, te_done, 2 * m)
                wait_alone(pool, "pool")
                rows = xn2_dram[0:KNOWN * S] if isinstance(m, int) and m < EARLY else xn2_dram
                for t in range(TH):
                    pool.indirect_dma_start(xg[:, t], None, rows,
                                            bass.IndirectOffsetOnAxis(ap=idx[:, t:t + 1], axis=0)
                                            ).then_inc(gathered, 16)

            def h_low(n, m):
                for k in range(2):
                    pool.wait_ge(h_his[n], 2 * m + k + 1)
                    pool.tensor_tensor(h_lo[n][:, 2 * k:2 * k + 2], h[n][:, 2 * k:2 * k + 2],
                                       h_hi[n][:, 2 * k:2 * k + 2].bitcast(F32), ALU.subtract).then_inc(h_los[n], 1)

            pipeline(pool, batch, *BATCHES)

            gather(1)
            send_tokens(B - 3)
            norm2_scale(B - 1)
            h_low(0, 0)
            gather(2)
            send_tokens(B - 2)
            h_low(1, 0)
            send_weights(B - 3)
            h_low(0, 1)
            gather(3)
            send_tokens(B - 1)
            h_low(1, 1)
            send_weights(B - 2)
            h_low(0, 2)
            send_weights(B - 1)
            gather(4)

            def tile(j, left):
                if has_tile(0, left):
                    h_low(1, j)
                if has_tile(1, left):
                    h_low(0, j + 1)
                if has_tile(3, left):
                    gather(j + 3)

            tiles = tiles_in_use(pool)
            pool.wait_ge(xn2_out, 16 * B)
            tile_pipeline(pool, tile, tiles)

            for n in range(3, B * RC, 4):
                pool.wait_ge(res_copied, n // 4 + 1)
                row = x_all[:, n // RC, n % RC]
                pool.tensor_tensor(row, v_rows[:, (n // 4) % 2], row, ALU.add).then_inc(res_pool, 1)

        @block.scalar
        def _(act):
            def exp(m):
                need(act, nbias_ready, 2 * (m + 1))
                need(act, tp_done, m)
                for c in range(RC):
                    act.activation(pexp[:, c], bS[:, c * S:(c + 1) * S], ACT.Exp, bias=nbias[:, c:c + 1],
                                   scale=rn1[:, 2, c:c + 1], accum_out=ssum[:, c:c + 1]).then_inc(exp_done, 1)

            def xt_high(m):
                act.wait_ge(xt_in, 16 * (m + 1))
                need(act, qa_done, 2 * m)
                act.activation(xt_hi[:], xt_raw[:], ACT.Copy).then_inc(xt_his, 1)

            def v_high(m):
                need(act, pv_done, 2 * m)
                for k in range(RC):
                    need(act, v_done, 2 * m + k + 1)
                    act.activation(v_hi[:, k], bV[k][:], ACT.Copy).then_inc(v_his, 1)

            def context_high(m):
                need(act, c_in, 16 * (m + 1))
                need(act, v_done, 2 * m)
                act.activation(c_hi[:], c_raw[:], ACT.Copy).then_inc(c_his, 1)

            def pt_high(m):
                need(act, tp_done, m + 1)
                act.activation(pt_hi[:], bS[:].rearrange("p (c s) -> p c s", c=RC), ACT.Copy).then_inc(pt_his, 1)

            def gt_high(m):
                need(act, gate_done, m)
                for k in range(2):
                    need(act, tg_done, 2 * m + k + 1)
                    act.activation(gt_hi[:, 2 * k:2 * k + 2], bG[k][:].rearrange("p (c s) -> p c s", c=2),
                                   ACT.Copy).then_inc(gt_his, 1)

            def qa_high(m):
                need(act, sc_done, m)
                for k in range(2):
                    need(act, qa_done, 2 * m + k + 1)
                    act.activation(qa_hi[:, 2 * k:2 * k + 2], bQ[k][:].rearrange("p (c s) -> p c s", c=2),
                                   ACT.Copy).then_inc(qa_his, 1)

            def gate_exp(m):
                need(act, gmax_ready, 2 * (m + 1))
                act.activation(gexp[:], logit[:], ACT.Exp, bias=gmax[:, 1:2], accum_out=gsum[:, 0:1]
                               ).then_inc(gexp_done, 1)

            def norm2(m):
                need(act, ln2_small, 4 * (m + 1))
                need(act, tg_done, 2 * m)
                need(act, xn2_out, 16 * m)
                for c in range(RC):
                    act.activation(xn2[:, c], x_all[:, bass.ds(m, 1), c].rearrange("p a d -> p (a d)"),
                                   ACT.Identity, bias=rn2[:, 3, c:c + 1], scale=rn2[:, 1, c:c + 1]
                                   ).then_inc(xn2_ready, 1)

            def batch(b):
                if exists(b, B):
                    exp(b)
                if exists(b - 1, B):
                    norm2(b - 1)
                if exists(b, B):
                    v_high(b)
                if exists(b + 1, B):
                    context_high(b + 1)
                if exists(b, B):
                    pt_high(b)
                if exists(b - 1, B):
                    gt_high(b - 1)
                if exists(b + 1, B):
                    qa_high(b + 1)
                if exists(b - 1, B):
                    gate_exp(b - 1)
                if exists(b + 2, B):
                    xt_high(b + 2)

            for n in range(DC):
                act.wait_ge(s_wq_mean, n + 1)
                act.activation(wq_raw[:, n], wq_raw[:, n], ACT.Identity, bias=wq_mean[:, n, 1:2]).then_inc(s_wq_c, 1)
                act.wait_ge(s_wq_c, n + 1)
                act.activation(wq_hi[:, n], wq_raw[:, n], ACT.Copy).then_inc(s_wq_hi, 1)
            xt_high(0)
            act.wait_ge(s_wv_in, 16)
            act.activation(wv_hi[:], wv_raw[:], ACT.Copy).then_inc(s_wv_hi, 1)
            for n in range(DC):
                act.wait_ge(a_mm, n + 1)
                act.activation(a_hi[:, n], bA[n][:], ACT.Copy).then_inc(a_his, 1)
            act.wait_ge(s_small, 64)
            act.activation(tg_attn[:], g_raw[:, 0:1], ACT.Tanh).then_inc(s_tanh, 1)
            act.activation(tg_ffn[:], g_raw[:, 1:2], ACT.Tanh).then_inc(s_tanh, 1)
            act.wait_ge(s_gw_zero, 1)
            act.activation(gw[:, :, 0:E], gw_raw[:], ACT.Copy).then_inc(s_gw_hi, 1)
            pipeline(act, batch, *BATCHES)

            def split_w(n, m):
                act.wait_ge(w_in[n], 16 * (m + 1))
                need(act, l_done[n], 2 * m)
                act.activation(w_hi[n][:], w_raw[n][:], ACT.Copy).then_inc(w_his[n], 1)

            def relu(n, m):
                act.wait_ge(b_in[n], 16 * (m + 1))
                for oc in range(DC):
                    if oc % 2 == 0:
                        act.wait_ge(l_done[n], 2 * m + oc // 2 + 1)
                        need(act, h_los[n], 2 * (m - 1) + oc // 2 + 1)
                    act.activation(h[n][:, oc], bL[n][oc // 2][:, (oc % 2) * TILE:(oc % 2 + 1) * TILE], ACT.Relu,
                                   bias=bias[n][:, oc:oc + 1]).then_inc(relu_done[n], 1)

            def et_high(m):
                need(act, l_done[0], 2 * m)
                for k in range(2):
                    act.wait_ge(te_done, 2 * m + k + 1)
                    act.activation(et_hi[:, 2 * k:2 * k + 2], bT[k][:].rearrange("p (c s) -> p c s", c=2),
                                   ACT.Copy).then_inc(et_his, 1)

            exp(B - 1)
            norm2(B - 2)
            v_high(B - 1)
            pt_high(B - 1)
            gt_high(B - 2)
            et_high(0)
            split_w(0, 0)
            gate_exp(B - 2)
            split_w(1, 0)
            relu(0, 0)
            norm2(B - 1)
            et_high(1)
            gt_high(B - 1)
            split_w(0, 1)
            split_w(2, 0)
            relu(1, 0)
            gate_exp(B - 1)
            split_w(1, 1)
            relu(0, 1)
            split_w(0, 2)
            et_high(2)

            def tile(j, left):
                if has_tile(0, left):
                    split_w(2, j)
                    relu(1, j)
                if has_tile(1, left):
                    split_w(1, j + 1)
                    relu(0, j + 1)
                if has_tile(2, left):
                    split_w(0, j + 2)
                    et_high(j + 2)

            tile(1, AHEAD + 1)
            tile_pipeline(act, tile, tiles_in_use(act))

            for n in range(3, B * RC, 4):
                act.wait_ge(o_done, n + 1)
                need(act, res_pool, n // 4 - 1)
                act.activation(v_rows[:, (n // 4) % 2], bank[n % 8][:], ACT.Copy).then_inc(res_copied, 1)

        @block.vector
        def _(dve):
            dve.wait_ge(s_iota, 6)
            dve.tensor_copy(iota_e[:], iota_i[:]).then_inc(s_conv, 1)
            dve.tensor_copy(ebase[:], ebase_i[:]).then_inc(s_conv, 1)
            dve.tensor_copy(jidx[:], jidx_i[:]).then_inc(s_conv, 1)
            dve.tensor_copy(base[:, 0], ebase_i[:]).then_inc(s_conv, 1)
            dve.memset(gw[:].bitcast(F32), 0.0).then_inc(s_gw_zero, 1)
            dve.memset(v_sum[:], 0.0).then_inc(v_step, 1)
            dve.wait_ge(v_step, 1)
            dve.wait_ge(s_conv, 4)

            def stats(src_batch, st, mv, done, step_sem_base):
                wait_alone(dve, "dve")
                for c in range(RC):
                    dve.bn_stats(st[:, c], x_all[:, bass.ds(src_batch, 1), c].rearrange("p a d -> p (a d)")
                                 ).then_inc(bn_step, 1)
                dve.wait_ge(bn_step, step_sem_base + RC)
                wait_alone(dve, "dve")
                for c in range(RC):
                    dve.bn_aggr(mv[:, c], st[:, c]).then_inc(done, 1)

            def low(dst, src, hi, done):
                dve.tensor_tensor(dst, src, hi.bitcast(F32), ALU.subtract).then_inc(done, 1)

            def two(bk):
                return bk[:].rearrange("p (c s) -> p c s", c=2)

            def exp_bias(m):
                need(dve, sc_done, m + 1)
                dve.tensor_reduce(smax[:], bS[:].rearrange("p (c s) -> p c s", c=RC), AX_X, ALU.max
                                  ).then_inc(nbias_ready, 1)
                dve.wait_ge(nbias_ready, 2 * m + 1)
                need(dve, ln1_small, 4 * (m + 1))
                dve.tensor_tensor(nbias[:], smax[:], rn1[:, 3, :], ALU.mult).then_inc(nbias_ready, 1)

            def norm1_stats(m):
                need(dve, x_in, 16 * (m + 1))
                need(dve, ln1_small, 4 * m)
                stats(m, st1, mv1, ln1_stat, bn_before(m, True))

            def xt_low(m):
                need(dve, xt_his, m + 1)
                low(xt_lo[:], xt_raw[:], xt_hi[:], xt_los)

            def v_pt_low(m):
                for k in range(RC):
                    need(dve, v_his, 2 * m + k + 1)
                    low(v_lo[:, k], bV[k][:], v_hi[:, k], v_los)
                need(dve, pt_his, m + 1)
                low(pt_lo[:], two(bS), pt_hi[:], pt_los)

            def gt_low(m):
                for k in range(2):
                    need(dve, gt_his, 2 * m + k + 1)
                    low(gt_lo[:, 2 * k:2 * k + 2], two(bG[k]), gt_hi[:, 2 * k:2 * k + 2], gt_los)

            def slots(m):
                dve.wait_ge(rank_done, m + 1)
                dve.tensor_copy(ind24[:, bass.ds(m * S, S)], R_IND).then_inc(slot_step, 1)
                dve.tensor_tensor(base[:, 1], base[:, 0], R_TOT[:, 0:E], ALU.add).then_inc(slot_step, 1)
                dve.wait_ge(slot_step, NSTEP * m + 2)
                dve.tensor_tensor(full[:].rearrange("p c e -> p (c e)"), R_RANK,
                                  base[:].rearrange("p c e -> p (c e)"), ALU.add).then_inc(slot_step, 1)
                dve.wait_ge(slot_step, NSTEP * m + 3)
                dve.tensor_tensor(base[:, 0], base[:, 1], R_TOT[:, E:2 * E], ALU.add).then_inc(slot_step, 1)
                dve.tensor_tensor(prod[:], oh[:], full[:].unsqueeze(2).broadcast_to([P, RC, TOPK, E]), ALU.mult
                                  ).then_inc(slot_step, 1)
                dve.wait_ge(slot_step, NSTEP * m + 5)
                dve.tensor_reduce(pos[:], prod[:], AX_X, ALU.add).then_inc(slot_step, 1)
                dve.wait_ge(slot_step, NSTEP * m + 6)
                if buf(m) == 0:
                    need(dve, tok_sent, 16 * RC * TOPK * m)
                    need(dve, w_sent, 16 * RC * TOPK * m)
                dve.tensor_copy(slot_u[:, buf(m)], pos[:].rearrange("p c k -> p (c k)")).then_inc(slot_step, 1)
                dve.tensor_copy(tok_u[:, buf(m)], tokall[:, bass.ds(m * RC, RC)]).then_inc(slot_step, 1)
                dve.tensor_copy(w_out[:, buf(m)].rearrange("p (c k) -> p c k", c=RC), top[:, :, 0:TOPK]
                                ).then_inc(slot_step, 1)

            def qa_low(m):
                for k in range(2):
                    need(dve, qa_his, 2 * m + k + 1)
                    low(qa_lo[:, 2 * k:2 * k + 2], two(bQ[k]), qa_hi[:, 2 * k:2 * k + 2], qa_los)

            def gate_softmax(m):
                need(dve, gate_done, m + 1)
                dve.tensor_scalar(logit_low[:], R_LOGIT_LOW, gb[:, 0:1], None, ALU.add).then_inc(gate_step, 1)
                dve.wait_ge(gate_step, 3 * m + 1)
                dve.tensor_tensor(logit[:], R_LOGIT, logit_low[:], ALU.add).then_inc(gate_step, 1)
                dve.wait_ge(gate_step, 3 * m + 2)
                dve.tensor_reduce(gmax[:, 0:1], logit[:], AX_X, ALU.max).then_inc(gmax_ready, 1)
                dve.wait_ge(gmax_ready, 2 * m + 1)
                dve.tensor_scalar(gmax[:, 1:2], gmax[:, 0:1], -1.0, None, ALU.mult).then_inc(gmax_ready, 1)
                dve.wait_ge(gexp_done, m + 1)
                dve.reciprocal(gsum[:, 1:2], gsum[:, 0:1]).then_inc(gate_step, 1)
                dve.wait_ge(gate_step, 3 * m + 3)
                dve.tensor_scalar(probs[:], gexp[:], gsum[:, 1:2], None, ALU.mult).then_inc(probs_ready, 1)

            def attended(m):
                need(dve, exp_done, RC * (m + 1))
                dve.reciprocal(rsum[:], ssum[:]).then_inc(coef_ready, 1)
                dve.wait_ge(coef_ready, 2 * m + 1)
                dve.tensor_scalar(coef[:], rsum[:], tg_attn[:, 0:1], None, ALU.mult).then_inc(coef_ready, 1)
                dve.wait_ge(coef_ready, 2 * m + 2)
                for c in range(RC):
                    row = x_all[:, bass.ds(m, 1), c].rearrange("p a d -> p (a d)")
                    need(dve, pv_done, 2 * m + c + 1)
                    dve.scalar_tensor_tensor(out=row, in0=bV[c][:], scalar=coef[:, c:c + 1], in1=row,
                                             op0=ALU.mult, op1=ALU.add).then_inc(x2_done, 1)
                dve.wait_ge(x2_done, 2 * m + 2)
                need(dve, ln2_small, 4 * m)
                stats(m, st2, mv2, ln2_stat, bn_before(m, False))

            def two_best(m):
                need(dve, pt8_done, m + 1)
                dve.tensor_copy(pr[:].rearrange("p c e -> p (c e)"), R_PROB).then_inc(top_step, 1)
                dve.wait_ge(top_step, NTOP * m + 1)
                wait_alone(dve, "dve")
                for c in range(RC):
                    dve.max(top[:, c], pr[:, c]).then_inc(top_step, 1)
                dve.wait_ge(top_step, NTOP * m + 3)
                wait_alone(dve, "dve")
                for c in range(RC):
                    dve.max_index(topi[:, c], top[:, c], pr[:, c]).then_inc(top_step, 1)
                dve.wait_ge(top_step, NTOP * m + 5)
                dve.tensor_copy(topf[:], topi[:, :, 0:TOPK]).then_inc(top_step, 1)
                dve.wait_ge(top_step, NTOP * m + 6)
                dve.tensor_tensor(oh[:].rearrange("p c k e -> p (c k) e"),
                                  topf[:].rearrange("p c k -> p (c k)").unsqueeze(2).broadcast_to([P, RC * TOPK, E]),
                                  iota_e[:].unsqueeze(1).broadcast_to([P, RC * TOPK, E]), ALU.is_equal
                                  ).then_inc(top_step, 1)
                dve.wait_ge(top_step, NTOP * m + 7)
                for r in range(3):
                    dve.tensor_tensor(ind3[:, :, r], oh[:, :, 0], oh[:, :, 1], ALU.add).then_inc(top_step, 1)

            def batch(b):
                if exists(b, B):
                    exp_bias(b)
                if exists(b - 2, B):
                    two_best(b - 2)
                if exists(b + 1, B):
                    if not (isinstance(b, int) and b == BATCHES[0]):
                        xt_low(b + 1)
                    norm1_stats(b + 1)
                if exists(b, B):
                    v_pt_low(b)
                if exists(b - 1, B):
                    gt_low(b - 1)
                if exists(b - 2, B):
                    slots(b - 2)
                if exists(b + 1, B):
                    qa_low(b + 1)
                if exists(b - 1, B):
                    gate_softmax(b - 1)
                if exists(b, B):
                    attended(b)
                if isinstance(b, int) and b == KNOWN + 1:
                    early_table()

            def link(ins, done, step):
                step[0] += 1
                ins.then_inc(done, 1)
                dve.wait_ge(done, step[0])

            def tile_list(do, first, n, passed):
                do(dve.tensor_tensor_scan(cum[:], onesE[:], ntile[:], 0.0, ALU.mult, ALU.add))
                do(dve.tensor_tensor(le[:, 0:n], cum[:, 0:E - 1].unsqueeze(1).broadcast_to([P, n, E - 1]),
                                     jidx[:, 0:n].unsqueeze(2).broadcast_to([P, n, E - 1]), ALU.is_le))
                do(dve.tensor_reduce(tile_e[:, first:first + n], le[:, 0:n], AX_X, ALU.add))
                do(dve.tensor_tensor(lep[:, 0:n], le[:, 0:n],
                                     passed.unsqueeze(1).broadcast_to([P, n, E - 1]), ALU.mult))
                do(dve.tensor_reduce(tile_prev[:, 0:n], lep[:, 0:n], AX_X, ALU.add))
                do(dve.tensor_tensor(row1[:, 0:n], jidx[:, 0:n], tile_prev[:, 0:n], ALU.subtract))

            def write_table(do, first, n):
                rows = slice(first, first + n)
                do(dve.tensor_scalar(row2[:, 0:n], row1[:, 0:n], float(TILE), None, ALU.mult))
                do(dve.scalar_tensor_tensor(out=row3[:, 0:n], in0=tile_e[:, rows], scalar=float(REGION),
                                            in1=row2[:, 0:n], op0=ALU.mult, op1=ALU.add))
                do(dve.tensor_copy(table[:, rows, 0], tile_e[:, rows]))
                do(dve.tensor_copy(table[:, rows, 1], row3[:, 0:n]))
                do(dve.tensor_tensor(tile_onehot[:, :, rows], tile_e[:, rows].unsqueeze(1).broadcast_to([P, E, n]),
                                     iota_e[:].unsqueeze(2).broadcast_to([P, E, n]), ALU.is_equal))

            def early_table():
                step = [0]

                def do(ins):
                    link(ins, early_step, step)

                do(dve.tensor_tensor(cnt[:], base[:, 0], ebase[:], ALU.subtract))
                do(dve.tensor_copy(cnt_i[:, 0], cnt[:]))
                do(dve.tensor_scalar(cnt_i[:, 1], cnt_i[:, 0], TILE_SHIFT, None, ALU.arith_shift_right))
                do(dve.tensor_copy(ntile[:], cnt_i[:, 1]))
                tile_list(do, 0, EARLY, ntile[:, 0:E - 1])
                write_table(do, 0, EARLY)

            def full_table():
                step = [0]

                def do(ins):
                    link(ins, table_step, step)

                do(dve.tensor_reduce(before[:], tile_onehot[:, :, 0:EARLY], AX_X, ALU.add))
                do(dve.tensor_tensor(cnt[:], base[:, 0], ebase[:], ALU.subtract))
                do(dve.tensor_scalar(cnt_i[:, 0], cnt[:], float(TILE - 1), None, ALU.add))
                do(dve.tensor_scalar(cnt_i[:, 1], cnt_i[:, 0], TILE_SHIFT, None, ALU.arith_shift_right))
                do(dve.tensor_copy(ntile_all[:], cnt_i[:, 1]))
                do(dve.tensor_tensor(ntile[:], ntile_all[:], before[:], ALU.subtract))
                do(dve.tensor_tensor(passed[:], ntile_all[:, 0:E - 1], before[:, 1:E], ALU.subtract))
                tile_list(do, EARLY, NT - EARLY, passed[:])
                do(dve.tensor_scalar(row1[:, 0:NT - EARLY], row1[:, 0:NT - EARLY], before[:, 0:1], None, ALU.add))
                do(dve.tensor_scalar(extra[:], cum[:, E - 1:E], float(NT_MIN - EARLY), None, ALU.subtract))
                write_table(do, EARLY, NT - EARLY)

            def bn_before(m, first_norm):
                if first_norm:
                    seconds = m - 1 if not isinstance(m, int) else max(0, m - 1)
                    return RC * (m + seconds)
                firsts = m + 2 if not isinstance(m, int) else min(B, m + 2)
                return RC * (m + firsts)

            def wq_minus_mean(n):
                dve.wait_ge(s_wq_in[n], 16)
                dve.tensor_reduce(wq_mean[:, n, 0:1], wq_raw[:, n], AX_X, ALU.add).then_inc(s_wq_sum, 1)
                dve.wait_ge(s_wq_sum, n + 1)
                dve.tensor_scalar(wq_mean[:, n, 1:2], wq_mean[:, n, 0:1], -1.0 / D, None, ALU.mult).then_inc(s_wq_mean, 1)

            wq_minus_mean(0)
            for n in range(DC):
                dve.wait_ge(s_wk_in[n], 16)
                dve.tensor_copy(wk_hi[:, n], wk_raw[:, n]).then_inc(s_wk_hi, 1)
                dve.wait_ge(s_wk_hi, n + 1)
                low(wk_lo[:, n], wk_raw[:, n], wk_hi[:, n], s_wk_lo)
                dve.wait_ge(s_wq_hi, n + 1)
                low(wq_lo[:, n], wq_raw[:, n], wq_hi[:, n], s_wq_lo)
                if n + 1 < DC:
                    wq_minus_mean(n + 1)
            xt_low(0)
            for n in range(DC):
                dve.wait_ge(a_his, n + 1)
                low(a_lo[:, n], bA[n][:], a_hi[:, n], a_los)
            dve.wait_ge(s_wv_hi, 1)
            low(wv_lo[:], wv_raw[:], wv_hi[:], s_wv_lo)
            dve.wait_ge(s_gw_hi, 1)
            low(gw[:, :, GLO:GLO + E], gw_raw[:], gw[:, :, 0:E], s_gw_lo)
            dve.wait_ge(s_tanh, 2)
            pipeline(dve, batch, *BATCHES)

            def w_low(n, m):
                dve.wait_ge(w_his[n], m + 1)
                low(w_lo[n][:], w_raw[n][:], w_hi[n][:], w_los[n])

            def h_high(n, m):
                need(dve, l_done[n + 1], 2 * m)
                for k in range(2):
                    dve.wait_ge(relu_done[n], DC * m + 2 * k + 2)
                    dve.tensor_copy(h_hi[n][:, 2 * k:2 * k + 2], h[n][:, 2 * k:2 * k + 2]).then_inc(h_his[n], 1)

            def et_low(m):
                for k in range(2):
                    dve.wait_ge(et_his, 2 * m + k + 1)
                    low(et_lo[:, 2 * k:2 * k + 2], two(bT[k]), et_hi[:, 2 * k:2 * k + 2], et_los)

            def weighted_sum(m, left=AHEAD):
                dve.wait_ge(b_in[2], 16 * (m + 1))
                dve.wait_ge(wb_in, 16 * (m + 1))
                dve.tensor_scalar(nb3[:], bias[2][:], -1.0, None, ALU.mult).then_inc(wsum_step, 1)
                dve.tensor_reduce(wsum[:], wb[:], AX_X, ALU.add).then_inc(wsum_step, 1)
                dve.wait_ge(wsum_step, 2 * m + 2)
                for oc in range(DC):
                    if oc % 2 == 0:
                        dve.wait_ge(l_done[2], 2 * m + oc // 2 + 1)
                    z = bZ[oc][:, 0:TILE] if left == 1 else bL[2][oc // 2][:, (oc % 2) * TILE:(oc % 2 + 1) * TILE]
                    dve.scalar_tensor_tensor(out=junk[:].rearrange("p (h t) -> p h t", h=TH),
                                             in0=z.rearrange("p (h t) -> p h t", h=TH), scalar=nb3[:, oc:oc + 1],
                                             in1=wb[:].rearrange("p (t h) -> p h t", h=TH),
                                             op0=ALU.max, op1=ALU.mult,
                                             accum_out=acc[:, oc:oc + 1]).then_inc(tail_small, 1)
                    dve.wait_ge(tail_small, DC * m + oc + 1)
                need(dve, v_acc, 2 * m)
                dve.scalar_tensor_tensor(out=part[:], in0=bias[2][:], scalar=wsum[:, 0:1], in1=acc[:],
                                         op0=ALU.mult, op1=ALU.add).then_inc(part_done, 1)
                dve.wait_ge(part_done, m + 1)
                dve.tensor_tensor(v_add[:], part[:].unsqueeze(1).broadcast_to([P, E, DC]),
                                  tile_onehot[:, :, bass.ds(m, 1)].broadcast_to([P, E, DC]), ALU.mult
                                  ).then_inc(v_acc, 1)
                dve.wait_ge(v_acc, 2 * m + 1)
                dve.tensor_tensor(v_sum[:], v_sum[:], v_add[:], ALU.add).then_inc(v_acc, 1)

            exp_bias(B - 1)
            two_best(B - 3)
            slots(B - 3)
            v_pt_low(B - 1)
            gt_low(B - 2)
            et_low(0)
            w_low(0, 0)
            gate_softmax(B - 2)
            attended(B - 1)
            w_low(1, 0)
            h_high(0, 0)
            two_best(B - 2)
            et_low(1)
            gt_low(B - 1)
            slots(B - 2)
            w_low(0, 1)
            gate_softmax(B - 1)
            h_high(1, 0)
            w_low(2, 0)
            two_best(B - 1)
            h_high(0, 1)
            w_low(1, 1)
            slots(B - 1)
            w_low(0, 2)
            et_low(2)
            weighted_sum(0)
            w_low(2, 1)
            h_high(1, 1)
            full_table()
            w_low(1, 2)
            h_high(0, 2)
            w_low(0, 3)
            et_low(3)
            weighted_sum(1)

            def tile(j, left):
                if has_tile(0, left):
                    w_low(2, j)
                    h_high(1, j)
                if has_tile(1, left):
                    w_low(1, j + 1)
                    h_high(0, j + 1)
                if has_tile(2, left):
                    w_low(0, j + 2)
                    et_low(j + 2)
                if has_tile(0, left):
                    weighted_sum(j, left)

            tiles = tiles_in_use(dve)
            tile_pipeline(dve, tile, tiles)

            vstep = [1]

            def vlink(ins):
                vstep[0] += 1
                ins.then_inc(v_step, 1)
                dve.wait_ge(v_step, vstep[0])

            dve.wait_ge(v_acc, 2 * tiles)
            vlink(dve.tensor_scalar(vs[:], v_sum[:], tg_ffn[:, 0:1], None, ALU.mult))
            vlink(dve.tensor_copy(vs_part[:, 0], vs[:]))
            vlink(dve.tensor_tensor(vs_rest[:], vs[:], vs_part[:, 0], ALU.subtract))
            dve.tensor_copy(v3[:, :, 0], vs_part[:, 0].rearrange("p e c -> p c e")).then_inc(v_step, 1)
            vstep[0] += 1
            vlink(dve.tensor_copy(vs_part[:, 1], vs_rest[:]))
            dve.tensor_copy(v3[:, :, 1], vs_part[:, 1].rearrange("p e c -> p c e")).then_inc(v_step, 1)
            vstep[0] += 1
            vlink(dve.tensor_tensor(v3[:, :, 2], vs_rest[:].rearrange("p e c -> p c e"),
                                    vs_part[:, 1].rearrange("p e c -> p c e"), ALU.subtract))
            dve.wait_ge(vt_done, 1)
            dve.tensor_copy(v24[:], bank[0][0:3 * E, :]).then_inc(v24_ready, 1)

            for n in range(B * RC):
                if n % 4 != 3:
                    dve.wait_ge(o_done, n + 1)
                    row = x_all[:, n // RC, n % RC]
                    dve.tensor_tensor(row, bank[n % 8][:], row, ALU.add).then_inc(res_dve, 1)

        @block.tensor
        def _(pe):
            def split_product(out_ap, left, right, done=None):
                n = len(left[0])
                for i in range(n):
                    lh, ll, rh, rl = left[0][i], left[1][i], right[0][i], right[1][i]
                    pe.matmul(out_ap, lh, rh, start=(i == 0), stop=False)
                    pe.matmul(out_ap, lh, rl, start=False, stop=False)
                    last = pe.matmul(out_ap, ll, rh, start=False, stop=(i == n - 1))
                if done is not None:
                    last.then_inc(done, 1)

            def cols(hi, lo, a, width):
                return ([hi[:, c, a:a + width] for c in range(hi.shape[1])],
                        [lo[:, c, a:a + width] for c in range(lo.shape[1])])

            def transpose_rows(src, banks, done):
                for dc in range(DC):
                    for c in range(RC):
                        last = pe.transpose(banks[dc // 2][:, (dc % 2) * S + c * P:(dc % 2) * S + (c + 1) * P],
                                            src[:, c, dc * P:(dc + 1) * P], ident[:])
                    if dc % 2 == 1:
                        last.then_inc(done, 1)

            for c in range(DC):
                pe.wait_ge(s_wq_lo, c + 1)
                pe.wait_ge(s_wk_lo, c + 1)
                for n in range(DC):
                    rows = slice(n * P, (n + 1) * P)
                    pe.matmul(bA[n][:], wq_hi[:, c, rows], wk_hi[:, c], start=(c == 0), stop=False)
                    pe.matmul(bA[n][:], wq_hi[:, c, rows], wk_lo[:, c], start=False, stop=False)
                    last = pe.matmul(bA[n][:], wq_lo[:, c, rows], wk_hi[:, c], start=False, stop=(c == DC - 1))
                    if c == DC - 1:
                        last.then_inc(a_mm, 1)
            pe.wait_ge(s_pool_const, 5)
            pe.wait_ge(a_los, DC)

            def scores(m):
                need(pe, qa_los, 2 * (m + 1))
                need(pe, c_los, m + 1)
                need(pe, pt_los, m)
                for c in range(RC):
                    split_product(bS[:, c * S:(c + 1) * S], cols(qa_hi, qa_lo, c * P, P), cols(c_hi, c_lo, 0, S),
                                  sc_done if c == RC - 1 else None)

            def values(m, c):
                if isinstance(m, int) and m == 0:
                    pe.wait_ge(s_wv_lo, 1)
                    pe.wait_ge(c_los, 1)
                need(pe, x2_done, 2 * m)
                split_product(bV[c][:], cols(c_hi, c_lo, c * P, P), cols(wv_hi, wv_lo, 0, D), v_done)

            def ranks(m):
                need(pe, top_step, NTOP * (m + 1))
                ind = ind3[:, :, 0]
                pe.matmul(R_RANK, tri[:], ind, start=True, stop=True)
                pe.matmul(R_TOT, ones[:], ind, start=True, stop=True)
                for c in range(RC):
                    last = pe.transpose(bR[0:3 * E, c * P:(c + 1) * P],
                                        ind3[:, c].rearrange("p r e -> p (r e)"), ident[:])
                last.then_inc(rank_done, 1)

            def pt_transposes(m):
                need(pe, exp_done, RC * (m + 1))
                for k in range(RC):
                    for c in range(RC):
                        last = pe.transpose(bS[:, k * S + c * P:k * S + (c + 1) * P],
                                            pexp[:, c, k * P:(k + 1) * P], ident[:])
                last.then_inc(tp_done, 1)

            def xn2_transposes(m):
                need(pe, xn2_ready, RC * (m + 1))
                need(pe, gt_los, 2 * m)
                transpose_rows(xn2, bG, tg_done)

            def x_times_a(m):
                need(pe, xt_los, m + 1)
                need(pe, qa_los, 2 * m)
                for n in range(DC):
                    split_product(bQ[n // 2][:, (n % 2) * S:(n % 2 + 1) * S], cols(a_hi, a_lo, n * P, P),
                                  cols(xt_hi, xt_lo, 0, S), qa_done if n % 2 == 1 else None)

            def gate_logits(m):
                if isinstance(m, int) and m == 0:
                    pe.wait_ge(s_gw_lo, 1)
                need(pe, gt_los, 2 * (m + 1))
                need(pe, slot_step, NSTEP * (m - 1) + 4)
                pe.matmul(bR[0:GLO + E, 0:S], gw[:, 0], gt_hi[:, 0], start=True, stop=False)
                for i in range(DC):
                    pe.matmul(R_LOGIT, gw[:, i, 0:E], gt_lo[:, i], start=False, stop=False)
                for i in range(1, DC):
                    last = pe.matmul(bR[0:GLO + E, 0:S], gw[:, i], gt_hi[:, i], start=False, stop=(i == DC - 1))
                last.then_inc(gate_done, 1)

            def p_times_v(m):
                need(pe, pt_los, m + 1)
                need(pe, v_los, 2 * (m + 1))
                for c in range(RC):
                    split_product(bV[c][:], cols(pt_hi, pt_lo, c * P, P), cols(v_hi, v_lo, 0, D), pv_done)

            def gate_transposes(m):
                need(pe, probs_ready, m + 1)
                wait_alone(pe, "pe")
                for c in range(RC):
                    last = pe.transpose(R_PROB[:, c * E:(c + 1) * E], probs[:, c * P:(c + 1) * P],
                                        ident[0:E, 0:E])
                last.then_inc(pt8_done, 1)

            def batch(b):
                if exists(b, B):
                    scores(b)
                if exists(b - 2, B):
                    gate_transposes(b - 2)
                if exists(b, B):
                    for c in range(1 if isinstance(b, int) and b == 0 else 0, RC):
                        values(b, c)
                if exists(b - 2, B):
                    ranks(b - 2)
                if exists(b, B):
                    pt_transposes(b)
                if exists(b - 1, B):
                    xn2_transposes(b - 1)
                if exists(b + 1, B):
                    x_times_a(b + 1)
                if isinstance(b, int) and b == BATCHES[0]:
                    values(0, 0)
                if exists(b - 1, B):
                    gate_logits(b - 1)
                if exists(b, B):
                    p_times_v(b)

            pipeline(pe, batch, *BATCHES)

            def layer_half(n, m, k):
                src_hi, src_lo = (et_hi, et_lo) if n == 0 else (h_hi[n - 1], h_lo[n - 1])
                for oc in range(2 * k, 2 * k + 2):
                    split_product(bL[n][k][:, (oc % 2) * TILE:(oc % 2 + 1) * TILE],
                                  cols(w_hi[n], w_lo[n], oc * P, P), cols(src_hi, src_lo, 0, TILE),
                                  l_done[n] if oc % 2 == 1 else None)

            def layer1_half(m, k):
                need(pe, w_los[0], m + 1)
                need(pe, et_los, 2 * (m + 1))
                need(pe, relu_done[0], DC * m)
                if isinstance(m, int) and m == 0 and k == 1:
                    need(pe, x2_done, RC * B - 1)
                layer_half(0, m, k)

            def layer2_half(m, k):
                if isinstance(m, int) and m == 0:
                    need(pe, x2_done, RC * B)
                    if k == 1:
                        need(pe, gt_los, 2 * B)
                need(pe, w_los[1], m + 1)
                need(pe, h_los[0], 2 * (m + 1))
                need(pe, relu_done[1], DC * m)
                layer_half(1, m, k)

            def layer3_half(m, k):
                need(pe, w_los[2], m + 1)
                need(pe, h_los[1], 2 * (m + 1))
                need(pe, part_done, m)
                if isinstance(m, int) and m == 0 and k == 1:
                    need(pe, slot_step, NSTEP * (B - 1) + 4)
                layer_half(2, m, k)

            def layer3_by_parts(m):
                need(pe, w_los[2], m + 1)
                need(pe, part_done, m)
                for i in range(DC):
                    if i % 2 == 0:
                        need(pe, h_los[1], 2 * m + i // 2 + 1)
                    for oc in range(DC):
                        z = bZ[oc][:, 0:TILE]
                        rows = slice(oc * P, (oc + 1) * P)
                        pe.matmul(z, w_hi[2][:, i, rows], h_hi[1][:, i], start=(i == 0), stop=False)
                        pe.matmul(z, w_hi[2][:, i, rows], h_lo[1][:, i], start=False, stop=False)
                        last = pe.matmul(z, w_lo[2][:, i, rows], h_hi[1][:, i], start=False, stop=(i == DC - 1))
                        if i == DC - 1 and oc % 2 == 1:
                            last.then_inc(l_done[2], 1)

            def row_transposes(m):
                need(pe, gathered, 16 * TH * (m + 1))
                need(pe, et_los, 2 * m)
                transpose_rows(xg, bT, te_done)

            scores(B - 1)
            gate_transposes(B - 3)
            values(B - 1, 0)
            ranks(B - 3)
            values(B - 1, 1)
            pt_transposes(B - 1)
            xn2_transposes(B - 2)
            need(pe, qa_los, 2 * B)
            row_transposes(0)
            gate_logits(B - 2)
            p_times_v(B - 1)
            layer1_half(0, 0)
            gate_transposes(B - 2)
            layer1_half(0, 1)
            row_transposes(1)
            xn2_transposes(B - 1)
            ranks(B - 2)
            layer2_half(0, 0)
            gate_logits(B - 1)
            layer2_half(0, 1)
            layer1_half(1, 0)
            gate_transposes(B - 1)
            layer1_half(1, 1)
            row_transposes(2)
            layer3_half(0, 0)
            ranks(B - 1)
            layer3_half(0, 1)

            def tile(j, left):
                if has_tile(0, left):
                    layer2_half(j, 0)
                    layer2_half(j, 1)
                if has_tile(1, left):
                    layer1_half(j + 1, 0)
                    layer1_half(j + 1, 1)
                if has_tile(2, left):
                    row_transposes(j + 2)
                if left == 1:
                    layer3_by_parts(j)
                else:
                    layer3_half(j, 0)
                    layer3_half(j, 1)

            tile(1, AHEAD + 1)
            tile_pipeline(pe, tile, tiles_in_use(pe))

            pe.wait_ge(v_step, 1 + 7)
            for c in range(DC):
                last = pe.transpose(bank[0][0:3 * E, c * P:(c + 1) * P],
                                    v3[:, c].rearrange("p r e -> p (r e)"), ident[:])
            last.then_inc(vt_done, 1)
            pe.wait_ge(v24_ready, 1)
            for n in range(B * RC):
                if n >= 8 and n % 4 == 3:
                    pe.wait_ge(res_copied, (n - 8) // 4 + 1)
                elif n >= 8:
                    pe.wait_ge(res_dve, n - 7 - (n - 7) // 4)
                pe.matmul(bank[n % 8][:], ind24[:, n * P:(n + 1) * P], v24[:], start=True, stop=True
                          ).then_inc(o_done, 1)


def _chunks(a):
    lead = a.shape[:-2]
    a = a.reshape(*lead, a.shape[-2] // P, P, a.shape[-1])
    return np.ascontiguousarray(np.swapaxes(a, -3, -2))


def kernel(x, ctx_1024, g_xattn, g_ffn, L0_xattn_Wq, L0_xattn_Wkv, L0_ffn_gate_w, L0_ffn_gate_b,
           L0_ffn_w1, L0_ffn_b1, L0_ffn_w2, L0_ffn_b2, L0_ffn_w3, L0_ffn_b3):
    import concourse.bacc as _bacc
    from concourse.bass_utils import run_bass_kernel_spmd as _run

    wkv = np.asarray(L0_xattn_Wkv)
    arrays = {
        "x": np.ascontiguousarray(x),
        "x_t": _chunks(np.swapaxes(np.asarray(x), 1, 2)),
        "ctx_t": _chunks(np.swapaxes(np.asarray(ctx_1024), 1, 2)),
        "g_xattn": np.ascontiguousarray(g_xattn),
        "g_ffn": np.ascontiguousarray(g_ffn),
        "wq_t": _chunks(np.asarray(L0_xattn_Wq).T),
        "wk_t": _chunks(wkv[:, :D].T),
        "wv": _chunks(wkv[:, D:]),
        "gate_w": _chunks(np.asarray(L0_ffn_gate_w)),
        "gate_b": np.ascontiguousarray(L0_ffn_gate_b),
        "w1": _chunks(np.asarray(L0_ffn_w1)),
        "w2": _chunks(np.asarray(L0_ffn_w2)),
        "w3": _chunks(np.asarray(L0_ffn_w3)),
        "b1": np.ascontiguousarray(np.swapaxes(np.asarray(L0_ffn_b1).reshape(E, DC, P), 1, 2)),
        "b2": np.ascontiguousarray(np.swapaxes(np.asarray(L0_ffn_b2).reshape(E, DC, P), 1, 2)),
        "b3": np.ascontiguousarray(np.swapaxes(np.asarray(L0_ffn_b3).reshape(E, DC, P), 1, 2)),
    }
    nc = _bacc.Bacc("TRN2", target_bir_lowering=False, num_devices=1)
    args = [nc.dram_tensor(f"in_{k}", a.shape, F32, kind="ExternalInput").ap() for k, a in arrays.items()]
    out = nc.dram_tensor("out", (B, S, D), F32, kind="ExternalOutput").ap()
    xn2_dram = nc.dram_tensor("xn2_dram", (TOK, D), F32).ap()
    slot_tok = nc.dram_tensor("slot_tok", (NSLOT, 1), U32).ap()
    slot_w = nc.dram_tensor("slot_w", (NSLOT, 1), F32).ap()
    flamingo_block(nc, *args, out, xn2_dram, slot_tok, slot_w)
    r = _run(nc, [{f"in_{k}": a for k, a in arrays.items()}], core_ids=[0])
    return r.results[0]["out"]
```
